# Optimizing a Trainium2 kernel written in Bass

```python
import numpy as np
import jax
import jax.numpy as jnp

def _softmax(x, axis=-1):
    return jax.nn.softmax(x, axis=axis)

def _gelu(x):
    return jax.nn.gelu(x, approximate=True)

def _silu(x):
    return jax.nn.silu(x)

def _sigmoid(x):
    return jax.nn.sigmoid(x)

def _layernorm(x, axis=-1, eps=1e-05):
    m = jnp.mean(x, axis=axis, keepdims=True)
    v = jnp.var(x, axis=axis, keepdims=True)
    return (x - m) / jnp.sqrt(v + eps)

def _scatter_add(tgt, idx, src, axis=0):
    return tgt.at[idx].add(src)

def _segment_sum(src, seg, n):
    return jax.ops.segment_sum(src, seg, n)
kernel_name = 'mk_decoder_postln_d1_seqx_r8_446e17'

def setup_inputs(seed: int=0):
    np.random.seed(seed)
    _w = jnp.asarray

    def _rec_inputs():
        import jax
        import jax.numpy as jnp
        _rk = jax.random.key(seed)
        x = -0.0003929 + 0.9999 * jax.random.normal(jax.random.fold_in(_rk, 1), (4, 256, 512), jnp.float32)
        _lenS = 256 - jax.random.randint(jax.random.fold_in(_rk, 7), (4,), 0, max(1, 256 // 4) + 1, jnp.int32)
        _lenS2 = 1601 - jax.random.randint(jax.random.fold_in(_rk, 8), (4,), 0, max(1, 1601 // 4) + 1, jnp.int32)
        _ctx_4096P = jax.random.normal(jax.random.fold_in(_rk, 11), (4, 16, 512), jnp.float32)
        _ctx_4096c = jax.random.dirichlet(jax.random.fold_in(_rk, 511), 0.3 * jnp.ones((16,), jnp.float32), (4, 1601))
        _ctx_4096t = jnp.einsum('bsk,bkd->bsd', _ctx_4096c, _ctx_4096P)
        _ctx_4096t = _ctx_4096t * jax.lax.rsqrt(jnp.mean(jnp.square(_ctx_4096t)) + 1e-12) * 0.953939
        ctx_4096 = 2.81802e-05 + 1.00001 * (_ctx_4096t + 0.3 * jax.random.normal(jax.random.fold_in(_rk, 611), (4, 1601, 512), jnp.float32))
        return (x, ctx_4096)
    x, ctx_4096 = _rec_inputs()

    def _L0_attn_setup():
        import jax, jax.numpy as jnp
        import numpy as np
        import math
        D_MODEL = 512
        N_HEADS = 32
        D_HEAD = D_MODEL // N_HEADS
        SEQ = 256
        BATCH = 1

        def rope(x):
            S = x.shape[2]
            D = x.shape[-1]
            theta = 1.0 / 10000.0 ** (jnp.arange(0, D, 2, dtype=jnp.float32) / D)
            ang = jnp.arange(S, dtype=jnp.float32)[:, None] * theta[None, :]
            cos = jnp.cos(ang)
            sin = jnp.sin(ang)
            x_even = x[..., ::2]
            x_odd = x[..., 1::2]
            rot_even = x_even * cos - x_odd * sin
            rot_odd = x_even * sin + x_odd * cos
            return jnp.stack((rot_even, rot_odd), axis=-1).reshape(x.shape)
        key = jax.random.key(seed)
        ks = jax.random.split(key, 9)
        scale = 1.0 / math.sqrt(D_MODEL)
        return {'x': jax.random.normal(ks[0], (BATCH, SEQ, D_MODEL), dtype=jnp.float32), 'Wq': jax.random.normal(ks[1], (D_MODEL, D_MODEL), dtype=jnp.float32) * scale, 'bq': jnp.zeros((D_MODEL,), dtype=jnp.float32), 'Wk': jax.random.normal(ks[2], (D_MODEL, D_MODEL), dtype=jnp.float32) * scale, 'bk': jnp.zeros((D_MODEL,), dtype=jnp.float32), 'Wv': jax.random.normal(ks[3], (D_MODEL, D_MODEL), dtype=jnp.float32) * scale, 'bv': jnp.zeros((D_MODEL,), dtype=jnp.float32), 'Wo': jax.random.normal(ks[4], (D_MODEL, D_MODEL), dtype=jnp.float32) * scale, 'bo': jnp.zeros((D_MODEL,), dtype=jnp.float32)}
    _L0_attn_all = _L0_attn_setup()
    _L0_attn_in = {k: v for k, v in _L0_attn_all.items() if k in ('Wq', 'bq', 'Wk', 'bk', 'Wv', 'bv', 'Wo', 'bo')}
    del _L0_attn_all

    def _L0_xattn_setup():
        import jax, jax.numpy as jnp
        import numpy as np
        HID = 512
        NHEAD = 32
        NKV = 8
        HDIM = 128
        G = NHEAD // NKV
        key = jax.random.key(seed)
        ks = jax.random.split(key, 6)
        s = 0.02
        B, L = (2, 256)
        return {'query': jax.random.normal(ks[0], (B, L, HID), jnp.float32), 'kv': jax.random.normal(ks[1], (B, L, HID), jnp.float32), 'Wq': jax.random.normal(ks[2], (HID, NHEAD * HDIM), jnp.float32) * s, 'bq': jnp.zeros((NHEAD * HDIM,), jnp.float32), 'Wkv': jax.random.normal(ks[3], (HID, 2 * NKV * HDIM), jnp.float32) * s, 'bkv': jnp.zeros((2 * NKV * HDIM,), jnp.float32), 'Wo': jax.random.normal(ks[4], (NHEAD * HDIM, HID), jnp.float32) * s, 'bo': jnp.zeros((HID,), jnp.float32)}
    _L0_xattn_all = _L0_xattn_setup()
    _L0_xattn_in = {k: v for k, v in _L0_xattn_all.items() if k in ('Wq', 'bq', 'Wkv', 'bkv', 'Wo', 'bo')}
    del _L0_xattn_all

    def _L0_ffn_setup():
        import jax, jax.numpy as jnp
        import numpy as np
        N_EXPERTS = 28
        TOP_K = 2
        RANK = 8
        LORA_ALPHA = 16
        SCALING = LORA_ALPHA / RANK
        TEMP = 1.0
        key = jax.random.key(seed)
        ks = jax.random.split(key, 5)
        B, S, D_IN, D_OUT = (4, 256, 512, 512)
        x = jax.random.normal(ks[0], (B, S, D_IN), dtype=jnp.float32)
        base_W = jax.random.normal(ks[1], (D_OUT, D_IN), dtype=jnp.float32) * (1.0 / np.sqrt(D_IN))
        gate_W = jax.random.normal(ks[2], (N_EXPERTS, D_IN), dtype=jnp.float32) * (1.0 / np.sqrt(D_IN))
        lora_A = jax.random.normal(ks[3], (N_EXPERTS, RANK, D_IN), dtype=jnp.float32) * (1.0 / np.sqrt(D_IN))
        lora_B = jax.random.normal(ks[4], (N_EXPERTS, D_OUT, RANK), dtype=jnp.float32) * 0.01
        return {'x': x, 'base_W': base_W, 'gate_W': gate_W, 'lora_A': lora_A, 'lora_B': lora_B}
    _L0_ffn_all = _L0_ffn_setup()
    _L0_ffn_in = {k: v for k, v in _L0_ffn_all.items() if k in ('base_W', 'gate_W', 'lora_A', 'lora_B')}
    del _L0_ffn_all
    return {'x': x, 'ctx_4096': ctx_4096, 'L0_attn_Wq': _L0_attn_in['Wq'], 'L0_attn_bq': _L0_attn_in['bq'], 'L0_attn_Wk': _L0_attn_in['Wk'], 'L0_attn_bk': _L0_attn_in['bk'], 'L0_attn_Wv': _L0_attn_in['Wv'], 'L0_attn_bv': _L0_attn_in['bv'], 'L0_attn_Wo': _L0_attn_in['Wo'], 'L0_attn_bo': _L0_attn_in['bo'], 'L0_xattn_Wq': _L0_xattn_in['Wq'], 'L0_xattn_bq': _L0_xattn_in['bq'], 'L0_xattn_Wkv': _L0_xattn_in['Wkv'], 'L0_xattn_bkv': _L0_xattn_in['bkv'], 'L0_xattn_Wo': _L0_xattn_in['Wo'], 'L0_xattn_bo': _L0_xattn_in['bo'], 'L0_ffn_base_W': _L0_ffn_in['base_W'], 'L0_ffn_gate_W': _L0_ffn_in['gate_W'], 'L0_ffn_lora_A': _L0_ffn_in['lora_A'], 'L0_ffn_lora_B': _L0_ffn_in['lora_B']}

def reference(x, ctx_4096, L0_attn_Wq, L0_attn_bq, L0_attn_Wk, L0_attn_bk, L0_attn_Wv, L0_attn_bv, L0_attn_Wo, L0_attn_bo, L0_xattn_Wq, L0_xattn_bq, L0_xattn_Wkv, L0_xattn_bkv, L0_xattn_Wo, L0_xattn_bo, L0_ffn_base_W, L0_ffn_gate_W, L0_ffn_lora_A, L0_ffn_lora_B):
    import jax
    import jax.numpy as jnp

    def _L0_attn_ref(x, Wq, bq, Wk, bk, Wv, bv, Wo, bo):
        import jax, jax.numpy as jnp
        import numpy as np
        import math
        D_MODEL = 512
        N_HEADS = 32
        D_HEAD = D_MODEL // N_HEADS
        SEQ = 256
        BATCH = 1

        def rope(x):
            S = x.shape[2]
            D = x.shape[-1]
            theta = 1.0 / 10000.0 ** (jnp.arange(0, D, 2, dtype=jnp.float32) / D)
            ang = jnp.arange(S, dtype=jnp.float32)[:, None] * theta[None, :]
            cos = jnp.cos(ang)
            sin = jnp.sin(ang)
            x_even = x[..., ::2]
            x_odd = x[..., 1::2]
            rot_even = x_even * cos - x_odd * sin
            rot_odd = x_even * sin + x_odd * cos
            return jnp.stack((rot_even, rot_odd), axis=-1).reshape(x.shape)
        B, S, _ = x.shape

        def proj(W, b):
            h = x @ W.T + b
            return h.reshape(B, S, N_HEADS, D_HEAD).transpose(0, 2, 1, 3)
        Q = rope(proj(Wq, bq))
        K = rope(proj(Wk, bk))
        V = proj(Wv, bv)
        scores = jnp.einsum('bhqd,bhkd->bhqk', Q, K) / math.sqrt(D_HEAD)
        causal = jnp.tril(jnp.ones((S, S), dtype=bool))
        scores = jnp.where(causal[None, None], scores, jnp.float32(-jnp.inf))
        attn = jax.nn.softmax(scores, axis=-1)
        out = jnp.einsum('bhqk,bhkd->bhqd', attn, V)
        out = out.transpose(0, 2, 1, 3).reshape(B, S, N_HEADS * D_HEAD)
        return out @ Wo.T + bo

    def _L0_xattn_ref(query, kv, Wq, bq, Wkv, bkv, Wo, bo):
        import jax, jax.numpy as jnp
        import numpy as np
        HID = 512
        NHEAD = 32
        NKV = 8
        HDIM = 128
        G = NHEAD // NKV
        B, L, _ = query.shape
        Lk = kv.shape[1]
        scale = jnp.asarray(1.0 / np.sqrt(HDIM), query.dtype)
        q = (query @ Wq + bq).reshape(B, L, NKV, G, HDIM)
        k_, v_ = jnp.split(kv @ Wkv + bkv, 2, axis=-1)
        k = k_.reshape(B, Lk, NKV, HDIM)
        v = v_.reshape(B, Lk, NKV, HDIM)
        scores = jnp.einsum('blkgd,bmkd->bkglm', q, k) * scale
        attn = jax.nn.softmax(scores, axis=-1)
        o = jnp.einsum('bkglm,bmkd->blkgd', attn, v).reshape(B, L, NHEAD * HDIM)
        return o @ Wo + bo

    def _L0_ffn_ref(x, base_W, gate_W, lora_A, lora_B):
        import jax, jax.numpy as jnp
        import numpy as np
        N_EXPERTS = 28
        TOP_K = 2
        RANK = 8
        LORA_ALPHA = 16
        SCALING = LORA_ALPHA / RANK
        TEMP = 1.0
        B, S, D_in = x.shape
        xf = x.reshape(B * S, D_in)
        base = xf @ base_W.T
        logits = xf @ gate_W.T
        top_vals, top_idx = jax.lax.top_k(logits, TOP_K)
        top_probs = jax.nn.softmax(top_vals / TEMP, axis=-1)
        N = xf.shape[0]
        gate_full = jnp.zeros((N, N_EXPERTS), dtype=xf.dtype).at[jnp.arange(N)[:, None], top_idx].add(top_probs)
        h = jnp.einsum('nd,erd->ner', xf, lora_A)
        h = h * (gate_full * SCALING)[:, :, None]
        lora_out = jnp.einsum('ner,eor->no', h, lora_B)
        out = base + lora_out
        return out.reshape(B, S, -1)
    x = _layernorm(x + _L0_attn_ref(x, L0_attn_Wq, L0_attn_bq, L0_attn_Wk, L0_attn_bk, L0_attn_Wv, L0_attn_bv, L0_attn_Wo, L0_attn_bo), axis=-1)
    x = _layernorm(x + _L0_xattn_ref(x, ctx_4096, L0_xattn_Wq, L0_xattn_bq, L0_xattn_Wkv, L0_xattn_bkv, L0_xattn_Wo, L0_xattn_bo), axis=-1)
    x = _layernorm(x + _L0_ffn_ref(x, L0_ffn_base_W, L0_ffn_gate_W, L0_ffn_lora_A, L0_ffn_lora_B), axis=-1)
    return x

_drawn_inputs = setup_inputs


def setup_inputs(seed=0):
    import zlib

    import numpy as np

    out = dict(_drawn_inputs(seed))
    spreads = {'L0_attn_bq': (0.0, 0.521),
     'L0_attn_bk': (0.0, 0.554),
     'L0_attn_bv': (0.0, 0.1),
     'L0_attn_bo': (0.0, 0.1),
     'L0_xattn_bq': (0.0, 0.8),
     'L0_xattn_bkv': (0.0, 0.1),
     'L0_xattn_bo': (0.0, 0.1)}
    factors = {'L0_xattn_Wq': 3.083}
    for name, (base, spread) in spreads.items():
        noise = np.random.default_rng([zlib.crc32(name.encode()), seed]).standard_normal(out[name].shape)
        drawn = base * np.exp(spread * noise) if base else spread * noise
        out[name] = jnp.asarray(drawn.astype(out[name].dtype))
    for name, factor in factors.items():
        out[name] = (out[name] * factor).astype(out[name].dtype)
    return out
```

```python
from contextlib import ExitStack

import numpy as np

import concourse.bass as bass
from concourse import mybir

F32 = mybir.dt.float32
F32R = mybir.dt.float32r
BF16 = mybir.dt.bfloat16
U32 = mybir.dt.uint32
ALU = mybir.AluOpType
ACT = mybir.ActivationFunctionType
AX = mybir.AxisListType

P = 128
B, S, D = 4, 256, 512
DC = D // P
TB = S // P
NH, DH = 32, 16
HB = P // DH
NM = NH // HB
XH, XKV, XD = 32, 8, 128
G = XH // XKV
NP = XKV // 2
LK = 1601
KT = (LK + P - 1) // P
LAST = LK - (KT - 1) * P
LKP = LK + 1
NE, RANK = 28, 8
ER = NE * RANK
LORA_SCALING = 16 / 8
GA = NE + ER
EPS = 1e-5
NEG = -1.0e30
XSCALE = 1.0 / float(np.sqrt(XD))
SSCALE = 1.0 / float(np.sqrt(DH))

KCH = [(0, 400), (400, 400), (800, 400), (1200, 402)]
MCH = [((0, 400), (400, 400), 400), ((800, 402), (1200, 402), 401)]

PIECES = 4
CTX_PIECES = [(0, 400), (400, 800), (800, 1200), (1200, LK)]
WKV_AT = (3, 5, 7, 9)

JOBS = [("K", 0, j) for j in range(4)] + [("Q", 0, g) for g in range(G)] \
    + [("K", 1, j) for j in range(4)] + [("Q", 1, g) for g in range(G)] + [("V", 0, t) for t in range(KT)]
NJ = len(JOBS)
HALVES = 4
NT = HALVES * KT
QH = 2 * S
RING = 3
assert (NJ + NT) % RING == 0 and NT % 2 == 0
PAIRS = 8
MXU = HALVES * (PAIRS + 1) + 1
MAX_AT = (10, 12, 14, 16, 18, 20, 22, 24)
C_ID, C_HM, C_IOTA, C_EPS, C_BK, C_BV, C_BQ = 0, 128, 136, 164, 165, 173, 181
C_N = C_BQ + XH


def at(turn, per_turn, n):
    return turn * per_turn + (per_turn + n)


def build(nc, x, x_t, ctx_t, ws, wkv, wq, wo, bo_s, bo_x, wb, wga, wlb, rope, consts, bmask, out, nb=B):
    with ExitStack() as ctx:
        def sb(name, shape, dt=F32, stack=ctx):
            return stack.enter_context(nc.sbuf_tensor(name, shape, dt))

        def sem(name):
            return ctx.enter_context(nc.semaphore(name))

        cst = sb("cst", [P, C_N])
        ones = sb("ones", [P, P])
        identb = sb("identb", [P, P], BF16)
        maskb = sb("maskb", [P, P], BF16)
        negones = sb("negones", [4, P], F32R)
        blockm = sb("blockm", [4, 4, P])
        xres = sb("xres", [P, TB, D])
        xt = sb("xt", [P, DC, S])
        stats = sb("stats", [P, TB, 6])
        mv = sb("mv", [P, TB, 2])
        rstd = sb("rstd", [P, TB])
        ctxh = sb("ctxh", [P, DC, LKP], F32R)
        ctxl = sb("ctxl", [P, DC, LKP], F32R)
        stage = sb("stage", [P, DC * 512])
        wkvh = sb("wkvh", [P, DC, 512], F32R)
        wkvl = sb("wkvl", [P, DC, 512], F32R)
        ident = cst[:, C_ID:C_ID + P]

        with ExitStack() as st:
            wsb = sb("wsb", [P, 3077], stack=st)
            rp = sb("rp", [P, 2, S], stack=st)
            bos = sb("bos", [P, D], stack=st)
            qr = sb("qr", [P, S], stack=st)
            kr = sb("kr", [P, S], stack=st)
            t1 = sb("t1", [P, S], stack=st)
            t2 = sb("t2", [P, S], stack=st)
            qm = sb("qm", [P, 2, S], stack=st)
            vx = sb("vx", [P, TB, HB * (P + DH)], stack=st)
            pn = sb("pn", [P, 3, 384], stack=st)
            pt = sb("pt", [P, 2, 384], stack=st)
            nmx = sb("nmx", [P, 3, 2], stack=st)
            sm = sb("sm", [P, 3, 2], stack=st)
            rsm = sb("rsm", [P, 3, 2], stack=st)
            ots = sb("ots", [P, S], stack=st)
        with ExitStack() as st:
            wbt = sb("wbt", [P, DC, D], stack=st)
            wgat = sb("wgat", [P, DC, GA], stack=st)
            wlbt = sb("wlbt", [P, 2, D], stack=st)
            box = sb("box", [P, D], stack=st)
            lg = sb("lg", [P, TB, NE], stack=st)
            top8 = sb("top8", [P, TB, 8], stack=st)
            idx8 = sb("idx8", [P, TB, 8], U32, stack=st)
            idxf = sb("idxf", [P, TB, 8], stack=st)
            dv21 = sb("dv21", [P, TB], stack=st)
            e21 = sb("e21", [P, TB], stack=st)
            den1 = sb("den1", [P, TB], stack=st)
            p1 = sb("p1", [P, TB], stack=st)
            p1s = sb("p1s", [P, TB], stack=st)
            p2s = sb("p2s", [P, TB], stack=st)
            g1 = sb("g1", [P, TB, NE], stack=st)
            g2 = sb("g2", [P, TB, NE], stack=st)
            gate = sb("gate", [P, TB, NE], stack=st)
            hg = sb("hg", [P, TB, ER], stack=st)
            hgt = sb("hgt", [P, TB, 2, P], stack=st)
        kh = sb("kh", [P, 2, LKP], F32R)
        kl = sb("kl", [P, 2, LKP], F32R)
        vh = sb("vh", [P, KT, 256], F32R)
        vl = sb("vl", [P, KT, 256], F32R)
        qh = sb("qh", [P, 2, G * S], F32R)
        ql = sb("ql", [P, 2, G * S], F32R)
        wqb = sb("wqb", [P, DC, G * XD])
        wob = sb("wob", [P, 2, 2, D])
        p32 = sb("p32", [P, 2, QH])
        ph = sb("ph", [P, 2, QH], F32R)
        pl = sb("pl", [P, 2, QH], F32R)
        psm = sb("psm", [P, 2, QH])
        rden = sb("rden", [P, QH])
        ot = sb("ot", [P, 2 * G, S])
        shift = sb("shift", [4, 2, 4, P], F32R)
        mxp = sb("mxp", [P, 2, PAIRS])
        m4 = sb("m4", [P, 2, 4])

        bank = [ctx.enter_context(nc.psum_tensor(f"bank{i}", [P, 512], F32)) for i in range(RING)]
        mx = ctx.enter_context(nc.psum_tensor("mx", [P, 2, 512], F32))
        pv = ctx.enter_context(nc.psum_tensor("pv", [P, 2, 512], F32))
        dn = ctx.enter_context(nc.psum_tensor("dn", [P, 512], F32))
        s_bank = [mx[:, 0, :], mx[:, 1, :], bank[2][:, :]]

        c_ld, c_set, phase, passed = (sem(n) for n in ("c_ld", "c_set", "phase", "passed"))
        x_ld, f_ld, stage_ld, split, stored = (sem(n) for n in ("x_ld", "f_ld", "stage_ld", "split", "stored"))
        split_hi, split_lo, xr_ok = sem("split_hi"), sem("split_lo"), sem("xr_ok")
        ln, ln_sd, xt_ps, xt_ok = (sem(n) for n in ("ln", "ln_sd", "xt_ps", "xt_ok"))
        f_mm, f_v, f_e, f_t, f_tc, f_o = (sem(n) for n in ("f_mm", "f_v", "f_e", "f_t", "f_tc", "f_o"))
        w_ld, s_qkv, s_rope, s_vz = (sem(n) for n in ("w_ld", "s_qkv", "s_rope", "s_vz"))
        s_qm, s_sc, s_mx, s_exp, s_rs, s_pn = (sem(n) for n in ("s_qm", "s_sc", "s_mx", "s_exp", "s_rs", "s_pn"))
        s_tp, s_ptc, s_pv, s_ot, s_y, s_res = (sem(n) for n in ("s_tp", "s_ptc", "s_pv", "s_ot", "s_y", "s_res"))
        wq_ld, wo_ld, wo_used = sem("wq_ld"), [sem("wo_ld0"), sem("wo_ld1")], sem("wo_used")
        job, job_hi, job_lo = sem("job"), sem("job_hi"), sem("job_lo")
        mx_mm, mx_free, m4_ok, mt_mm, shift_ok = (sem(n) for n in ("mx_mm", "mx_free", "m4_ok", "mt_mm", "shift_ok"))
        sc_mm, exp_ok, hi_ok, lo_ok, sum_ok, pv_mm = (sem(n) for n in ("sc_mm", "exp_ok", "hi_ok", "lo_ok", "sum_ok", "pv_mm"))
        den_mm, rden_ok, on_ok, ot_ok = (sem(n) for n in ("den_mm", "rden_ok", "on_ok", "ot_ok"))

        N_STAGE = 4 + NP
        N_CONST = 2 * 16
        N_ROPE = 8
        N_LN = 9
        N_FV = 7 + 4 + 2 * TB + 1 + TB

        def held(eng):
            eng.sem_inc(passed, 1)

        def all_meet(eng, b, k):
            held(eng)
            eng.drain().then_inc(phase, 1)
            eng.wait_ge(phase, b * 15 + 5 * (k + 1))
            held(eng)

        block = ctx.enter_context(nc.Block())

        @block.sync
        def _(sp):
            sp.dma_start(cst[:, :], consts).then_inc(c_ld, 16)
            sp.dma_start(blockm[:, :, :], bmask).then_inc(c_ld, 16)
            for s_, n in ((x_ld, 64), (f_ld, 64), (stage_ld, 16 * N_STAGE), (w_ld, 16), (wq_ld, 32),
                          (wo_ld[0], 32), (wo_ld[1], 32), (stored, 16)):
                sp.sem_inc(s_, n)
            sp.dma_start(stage[:, :], wkv[0]).then_inc(stage_ld, 16)
            with sp.Fori(0, nb) as b:
                sp.dma_start(xres[:, :, :], x[b]).then_inc(x_ld, 16)
                sp.dma_start(xt[:, :, :], x_t[b]).then_inc(x_ld, 16)
                sp.dma_start(rp[:, :, :], rope).then_inc(x_ld, 16)
                sp.dma_start(bos[:, :], bo_s).then_inc(x_ld, 16)
                with sp.Fori(0, NM) as m:
                    t = b * NM + m
                    sp.wait_ge(s_y, at(t, 2, 0))
                    held(sp)
                    sp.wait_ge(s_ot, at(t, 1, 0))
                    held(sp)
                    sp.wait_ge(s_rope, at(t, N_ROPE, 0))
                    sp.dma_start(wsb[:, :], ws[m]).then_inc(w_ld, 16)
                    sp.wait_ge(split, at(b, N_STAGE, 1) + m)
                    sp.dma_start(stage[:, 0:LK], ctx_t[b, m]).then_inc(stage_ld, 16)
                all_meet(sp, b, 0)
                with sp.Fori(0, NP) as p:
                    t = b * NP + p
                    for kv in range(2):
                        sp.wait_ge(job, at(t, NJ, 0) if kv == 0 else at(t, NJ, 8))
                        sp.dma_start(wqb[:, :, :], wq[2 * p + kv]).then_inc(wq_ld, 16)
                    sp.wait_ge(split, at(b, N_STAGE, 5) + p)
                    sp.dma_start(stage[:, :], wkv[p + 1]).then_inc(stage_ld, 16)
                    for c in range(4):
                        sp.wait_ge(wo_used, at(t, 4, c - 1))
                        sp.dma_start(wob[:, c % 2, :, :], wo[4 * p + c]).then_inc(wo_ld[c % 2], 16)
                all_meet(sp, b, 1)
                sp.dma_start(wbt[:, :, :], wb).then_inc(f_ld, 16)
                sp.dma_start(wgat[:, :, :], wga).then_inc(f_ld, 16)
                sp.dma_start(wlbt[:, :, :], wlb).then_inc(f_ld, 16)
                sp.dma_start(box[:, :], bo_x).then_inc(f_ld, 16)
                sp.wait_ge(ln, at(b, 3 * N_LN, 3 * N_LN))
                sp.dma_start(out[b], xres[:, :, :]).then_inc(stored, 16)
                sp.wait_ge(stored, at(b, 16, 16))
                all_meet(sp, b, 2)

        @block.gpsimd
        def _(pool):
            nc.gpsimd.memset(ones[:, :], 1.0).then_inc(c_set, 1)
            nc.gpsimd.memset(negones[:, :].bitcast(F32), -1.0).then_inc(c_set, 1)
            nc.gpsimd.memset(ctxh[:, :, LK:LKP].bitcast(F32), 0.0).then_inc(c_set, 1)
            nc.gpsimd.memset(ctxl[:, :, LK:LKP].bitcast(F32), 0.0).then_inc(c_set, 1)
            nc.gpsimd.memset(identb[:, :], 0.0).then_inc(c_set, 1)
            nc.gpsimd.memset(maskb[:, :], 0.0).then_inc(c_set, 1)
            pool.wait_ge(c_set, 6)
            nc.gpsimd.affine_select(out=identb[:, :], in_=identb[:, :], compare_op=ALU.not_equal, fill=1.0,
                                    base=0, pattern=[[-1, P]], channel_multiplier=1).then_inc(c_set, 1)
            nc.gpsimd.affine_select(out=maskb[:, :], in_=maskb[:, :], compare_op=ALU.is_ge, fill=NEG,
                                    base=0, pattern=[[-1, P]], channel_multiplier=1).then_inc(c_set, 1)
            pool.sem_inc(split, N_STAGE)
            pool.sem_inc(sum_ok, HALVES * (KT - 1))
            wstage = stage[:, :].rearrange("p (c n) -> p c n", c=DC)

            def low_part(k, lo, hi, src, n):
                pool.wait_ge(split_hi, n * PIECES + k + 1)
                part = nc.gpsimd.tensor_tensor(lo, src, hi, ALU.subtract)
                part.then_inc(split_lo, 1)
                if k == PIECES - 1:
                    pool.wait_ge(split_lo, (n + 1) * PIECES)
                    pool.sem_inc(split, 1)

            for k in range(PIECES):
                low_part(k, wkvl[:, k, :], wkvh[:, k, :], wstage[:, k, :], 0)
            with pool.Fori(0, nb) as b:
                with pool.Fori(0, DC) as c:
                    for k, (a, z) in enumerate(CTX_PIECES):
                        low_part(k, ctxl[:, c, a:z], ctxh[:, c, a:z], stage[:, a:z], b * N_STAGE + c + 1)
                all_meet(pool, b, 0)
                with pool.Fori(0, NP) as p:
                    t = b * NP + p
                    for h in range(HALVES):
                        acc = psm[:, h % 2, :]
                        pool.wait_ge(den_mm, at(t, HALVES, h - 1))
                        for i in range(1, KT):
                            n = LAST if i == KT - 1 else P
                            g = h * KT + i
                            pool.wait_ge(exp_ok, at(t, NT, g + 1))
                            if i == 1:
                                add = nc.gpsimd.tensor_tensor(acc, p32[:, (g - 1) % 2, :], p32[:, g % 2, :], ALU.add)
                            else:
                                pool.wait_ge(sum_ok, at(t, HALVES * (KT - 1), h * (KT - 1) + i - 1))
                                add = nc.gpsimd.tensor_tensor(acc[0:n], acc[0:n], p32[0:n, g % 2, :], ALU.add)
                            add.then_inc(sum_ok, 1)
                            if h == 1 and i in WKV_AT:
                                k = WKV_AT.index(i)
                                low_part(k, wkvl[:, k, :], wkvh[:, k, :], wstage[:, k, :], b * N_STAGE + 5 + p)
                all_meet(pool, b, 1)
                all_meet(pool, b, 2)

        def sums_after(g):
            h, i = divmod(g, KT)
            return h * (KT - 1) + max(i, 1)

        def add_bv(act, t, p, h):
            act.wait_ge(on_ok, at(t, HALVES, h + 1))
            held(act)
            nc.scalar.activation(ot[:, 2 * h:2 * h + 2, :], ot[:, 2 * h:2 * h + 2, :], ACT.Identity,
                                 bias=cst[:, bass.ds(2 * p + (C_BV + h // 2), 1)]).then_inc(ot_ok, 1)

        @block.scalar
        def _(act):
            for s_, n in ((ln_sd, 3), (xt_ok, 4), (f_e, 1), (f_tc, 4), (s_exp, 2 * HB), (s_ptc, HB), (s_ot, 1),
                          (job_hi, NJ), (exp_ok, NT), (hi_ok, NT), (ot_ok, HALVES)):
                act.sem_inc(s_, n)
            act.wait_ge(c_ld, N_CONST)

            def deviation(b, k):
                act.wait_ge(ln, at(b, 3 * N_LN, N_LN * k + 6))
                nc.scalar.activation(rstd[:, :], mv[:, :, 1], ACT.Sqrt, bias=cst[:, C_EPS:C_EPS + 1]).then_inc(ln_sd, 1)

            def copy_xt(b, k):
                for tb in range(TB):
                    act.wait_ge(xt_ps, at(b, 2 * TB, TB * k + tb + 1))
                    nc.scalar.activation(xt[:, :, tb * P:(tb + 1) * P],
                                         bank[tb][:, :].rearrange("p (c n) -> p c n", c=DC), ACT.Copy).then_inc(xt_ok, 1)

            def high_part(hi, src):
                nc.scalar.activation(hi, src, ACT.Copy).then_inc(split_hi, 1)

            wstage = stage[:, :].rearrange("p (c n) -> p c n", c=DC)
            act.wait_ge(stage_ld, 16 * N_STAGE + 16)
            for k in range(PIECES):
                high_part(wkvh[:, k, :], wstage[:, k, :])

            with act.Fori(0, nb) as b:
                with act.Fori(0, NM) as m:
                    t = b * NM + m
                    act.wait_ge(s_y, at(t, 2, 0))
                    for h in range(HB + 2):
                        if h < HB:
                            act.wait_ge(s_mx, at(t, 2 * HB, 2 * h + 2))
                            act.wait_ge(s_tp, at(t, HB, h - 2))
                            act.wait_ge(s_rs, at(t, HB, h - 2))
                            for qb, (a, z) in enumerate(((0, 128), (128, 384))):
                                nc.scalar.activation(pn[:, h % 3, a:z], s_bank[h % 3][:, a:z], ACT.Exp,
                                                     bias=nmx[:, h % 3, qb:qb + 1],
                                                     accum_out=sm[:, h % 3, qb:qb + 1]).then_inc(s_exp, 1)
                        if h >= 2:
                            k = h - 2
                            act.wait_ge(s_tp, at(t, HB, k + 1))
                            act.wait_ge(s_pv, at(t, HB, k - 1))
                            nc.scalar.activation(pt[:, k % 2, :], pv[:, k % 2, 0:384], ACT.Copy).then_inc(s_ptc, 1)
                        if h in (1, 3, 5, 7):
                            if h == 1:
                                act.wait_ge(stage_ld, 16 * (b * N_STAGE + m) + 16 * (N_STAGE + 2))
                                held(act)
                            a, z = CTX_PIECES[h // 2]
                            high_part(ctxh[:, bass.ds(m, 1), a:z], stage[:, a:z].unsqueeze(1))
                    act.wait_ge(s_pv, at(t, HB, HB))
                    nc.scalar.activation(ots[:, :], dn[:, 0:S], ACT.Identity, bias=wsb[:, 3076:3077]).then_inc(s_ot, 1)
                deviation(b, 0)
                copy_xt(b, 0)
                all_meet(act, b, 0)
                with act.Fori(0, NP) as p:
                    t = b * NP + p
                    for j, (kind, kv, i) in enumerate(JOBS):
                        act.wait_ge(job, at(t, NJ, j + 1))
                        src = bank[j % RING]
                        if kind == "K":
                            a, n = KCH[i]
                            if i == 0 and kv == 0:
                                act.wait_ge(sc_mm, at(t, NT, 0))
                            held(act)
                            nc.scalar.activation(kh[:, kv, a:a + n], src[:, 0:n], ACT.Identity,
                                                 bias=cst[:, bass.ds(2 * p + (C_BK + kv), 1)]).then_inc(job_hi, 1)
                        elif kind == "Q":
                            held(act)
                            nc.scalar.activation(qh[:, kv, i * S:(i + 1) * S], src[:, 0:S], ACT.Identity,
                                                 bias=cst[:, bass.ds(8 * p + (C_BQ + G * kv + i), 1)]).then_inc(job_hi, 1)
                        else:
                            n = LAST if i == KT - 1 else P
                            if i == 0:
                                act.wait_ge(pv_mm, at(t, NT, 0))
                            nc.scalar.activation(vh[0:n, i, :], src[0:n, 0:256], ACT.Copy).then_inc(job_hi, 1)
                    for g in range(NT):
                        h, i = divmod(g, KT)
                        n = LAST if i == KT - 1 else P
                        act.wait_ge(sc_mm, at(t, NT, g + 1))
                        act.wait_ge(sum_ok, at(t, HALVES * (KT - 1), sums_after(g - 2)))
                        act.wait_ge(lo_ok, at(t, NT, g - 1))
                        nc.scalar.activation(p32[0:n, g % 2, :], bank[(NJ + g) % RING][0:n, :], ACT.Exp,
                                             scale=XSCALE).then_inc(exp_ok, 1)
                        act.wait_ge(exp_ok, at(t, NT, g + 1))
                        act.wait_ge(pv_mm, at(t, NT, g - 1))
                        nc.scalar.activation(ph[0:n, g % 2, :], p32[0:n, g % 2, :], ACT.Copy).then_inc(hi_ok, 1)
                        if h == 1 and i in WKV_AT:
                            k = WKV_AT.index(i)
                            if k == 0:
                                act.wait_ge(stage_ld, 16 * (b * N_STAGE + p) + 16 * (N_STAGE + 6))
                                act.wait_ge(job, at(t, NJ, NJ))
                            high_part(wkvh[:, k, :], wstage[:, k, :])
                        if i == KT - 1 and h >= 1:
                            add_bv(act, t, p, h - 1)
                    add_bv(act, t, p, HALVES - 1)
                all_meet(act, b, 1)
                deviation(b, 1)
                copy_xt(b, 1)
                act.wait_ge(f_v, at(b, N_FV, 7))
                nc.scalar.activation(e21[:, :], dv21[:, :], ACT.Exp).then_inc(f_e, 1)
                for tb in range(TB):
                    act.wait_ge(f_t, at(b, TB, tb + 1))
                    for k, n in enumerate((P, ER - P)):
                        nc.scalar.activation(hgt[0:n, tb, k, :], pv[0:n, tb, k * P:(k + 1) * P], ACT.Copy).then_inc(f_tc, 1)
                deviation(b, 2)
                all_meet(act, b, 2)

        @block.vector
        def _(dve):
            for s_, n in ((ln, 3 * N_LN), (f_v, N_FV), (s_rope, N_ROPE), (s_qm, HB), (s_mx, 2 * HB), (s_rs, HB),
                          (s_pn, 2 * HB), (s_res, 2), (job_lo, NJ), (mx_free, MXU), (m4_ok, HALVES),
                          (shift_ok, HALVES), (lo_ok, NT), (rden_ok, 4 * HALVES), (on_ok, HALVES)):
                dve.sem_inc(s_, n)
            dve.wait_ge(c_ld, N_CONST)

            def layernorm(b, k, add):
                def done(n):
                    dve.wait_ge(ln, at(b, 3 * N_LN, N_LN * k + n))
                for tb in range(TB):
                    add(tb).then_inc(ln, 1)
                done(2)
                for tb in range(TB):
                    nc.vector.bn_stats(stats[:, tb, :], xres[:, tb, :]).then_inc(ln, 1)
                done(4)
                held(dve)
                for tb in range(TB):
                    nc.vector.bn_aggr(mv[:, tb, :], stats[:, tb, :]).then_inc(ln, 1)
                dve.wait_ge(ln_sd, at(b, 3, k + 1))
                nc.vector.reciprocal(rstd[:, :], rstd[:, :]).then_inc(ln, 1)
                done(7)
                for tb in range(TB):
                    nc.vector.tensor_scalar(xres[:, tb, :], xres[:, tb, :], mv[:, tb, 0:1], rstd[:, tb:tb + 1],
                                            ALU.subtract, ALU.mult).then_inc(ln, 1)

            with dve.Fori(0, nb) as b:
                nc.vector.memset(vx[:, :, :], 0.0).then_inc(s_vz, 1)
                dve.wait_ge(s_vz, b + 1)
                dve.wait_ge(x_ld, at(b, 64, 64))
                held(dve)
                with dve.Fori(0, NM) as m:
                    t = b * NM + m
                    dve.wait_ge(w_ld, at(t, 16, 16))
                    dve.wait_ge(s_qm, at(t, HB, 0))
                    for k, (dst, base) in enumerate(((qr, 0), (kr, 1))):
                        dve.wait_ge(s_qkv, at(t, 3, k + 1))
                        if k == 0:
                            dve.wait_ge(s_rope, at(t, N_ROPE, 0))
                        else:
                            dve.wait_ge(s_rope, at(t, N_ROPE, 3))
                            dve.wait_ge(s_sc, at(t, HB, 0))
                        for q, (tmp, c0) in enumerate(((t1, 0), (t2, S))):
                            nc.vector.scalar_tensor_tensor(tmp[:, :], bank[k][:, c0:c0 + S],
                                                           wsb[:, 3072 + 2 * k + q:3073 + 2 * k + q], rp[:, q, :],
                                                           ALU.add, ALU.mult).then_inc(s_rope, 1)
                        dve.wait_ge(s_rope, at(t, N_ROPE, 3 * k + 2))
                        nc.vector.tensor_tensor(dst[:, :], t1[:, :], t2[:, :], ALU.add).then_inc(s_rope, 1)
                    dve.wait_ge(s_qkv, at(t, 3, 3))
                    dve.wait_ge(s_pv, at(t, HB, 0))
                    for tb in range(TB):
                        nc.vector.tensor_copy(vx[:, tb, :].rearrange("p (h x) -> p h x", h=HB)[:, :, 0:DH],
                                              bank[2][:, tb * P:(tb + 1) * P].rearrange("p (h x) -> p h x", h=HB)).then_inc(s_rope, 1)
                    dve.wait_ge(s_rope, at(t, N_ROPE, 3))

                    def one_head(h):
                        dve.wait_ge(s_sc, at(t, HB, h - 1))
                        nc.vector.tensor_scalar(qm[:, h % 2, :], qr[:, :], cst[:, C_HM + h:C_HM + h + 1], SSCALE,
                                                ALU.mult, ALU.mult).then_inc(s_qm, 1)
                    one_head(0)
                    one_head(1)
                    for h in range(HB + 1):
                        if h < HB:
                            dve.wait_ge(s_sc, at(t, HB, h + 1))
                            dve.wait_ge(s_exp, at(t, 2 * HB, 2 * h - 4))
                            for qb, (a, z) in enumerate(((0, 128), (128, 384))):
                                nc.vector.tensor_reduce(nmx[:, h % 3, qb:qb + 1], s_bank[h % 3][:, a:z], AX.X, ALU.max,
                                                        negate=True).then_inc(s_mx, 1)
                        if h + 2 < HB:
                            one_head(h + 2)
                        if h >= 1:
                            k = h - 1
                            dve.wait_ge(s_exp, at(t, 2 * HB, 2 * k + 2))
                            dve.wait_ge(s_pn, at(t, 2 * HB, 2 * k - 4))
                            nc.vector.reciprocal(rsm[:, k % 3, :], sm[:, k % 3, :]).then_inc(s_rs, 1)
                            dve.wait_ge(s_rs, at(t, HB, k + 1))
                            for qb, (a, z) in enumerate(((0, 128), (128, 384))):
                                nc.vector.tensor_scalar(pn[:, k % 3, a:z], pn[:, k % 3, a:z], rsm[:, k % 3, qb:qb + 1],
                                                        None, ALU.mult).then_inc(s_pn, 1)
                    for tb in range(TB):
                        dve.wait_ge(s_y, at(t, 2, tb + 1))
                        dve.wait_ge(s_res, at(t, 2, tb - 1))
                        nc.vector.tensor_tensor(xres[:, tb, :], xres[:, tb, :], bank[tb][:, :], ALU.add).then_inc(s_res, 1)
                dve.wait_ge(s_res, at(b * NM + (NM - 1), 2, 2))
                layernorm(b, 0, lambda tb: nc.vector.tensor_tensor(xres[:, tb, :], xres[:, tb, :], bos[:, :], ALU.add))
                all_meet(dve, b, 0)
                with dve.Fori(0, NP) as p:
                    t = b * NP + p

                    def reduce_pair(h, r):
                        k = h * (PAIRS + 1) + r
                        n = MCH[r % 2][2]
                        dve.wait_ge(mx_mm, at(t, HALVES * PAIRS, h * PAIRS + r + 1))
                        if r == 0:
                            dve.wait_ge(m4_ok, at(t, HALVES, h - 1))
                        nc.vector.tensor_reduce(mxp[:, h % 2, r:r + 1], mx[:, :, 0:n], AX.XY, ALU.max).then_inc(mx_free, 1)
                        assert k < MXU

                    def whole_max(h):
                        dve.wait_ge(mx_free, at(t, MXU, h * (PAIRS + 1) + PAIRS))
                        dve.wait_ge(mt_mm, at(t, HALVES, h - 1))
                        nc.vector.tensor_reduce(m4[:, h % 2, :], mxp[:, h % 2, :].rearrange("p (a c) -> p a c", c=2),
                                                AX.X, ALU.max).then_inc(m4_ok, 1)

                    def make_shift(h):
                        dve.wait_ge(mt_mm, at(t, HALVES, h + 1))
                        dve.wait_ge(sc_mm, at(t, NT, (h - 1) * KT))
                        nc.vector.tensor_tensor(shift[:, h % 2, :, :], blockm[:, :, :],
                                                mx[0:4, 0:1, 0:P].broadcast_to([4, 4, P]), ALU.mult).then_inc(shift_ok, 1)
                        dve.wait_ge(shift_ok, at(t, HALVES, h + 1))
                        dve.sem_inc(mx_free, 1)

                    for j, (kind, kv, i) in enumerate(JOBS):
                        if j in MAX_AT:
                            reduce_pair(0, MAX_AT.index(j))
                        dve.wait_ge(job_hi, at(t, NJ, j + 1))
                        src = bank[j % RING]
                        if kind == "K":
                            a, n = KCH[i]
                            nc.vector.scalar_tensor_tensor(kl[:, kv, a:a + n], src[:, 0:n],
                                                           cst[:, bass.ds(2 * p + (C_BK + kv), 1)],
                                                           kh[:, kv, a:a + n], ALU.add, ALU.subtract).then_inc(job_lo, 1)
                        elif kind == "Q":
                            nc.vector.scalar_tensor_tensor(ql[:, kv, i * S:(i + 1) * S], src[:, 0:S],
                                                           cst[:, bass.ds(8 * p + (C_BQ + G * kv + i), 1)],
                                                           qh[:, kv, i * S:(i + 1) * S], ALU.add, ALU.subtract).then_inc(job_lo, 1)
                        else:
                            n = LAST if i == KT - 1 else P
                            nc.vector.tensor_tensor(vl[0:n, i, :], src[0:n, 0:256], vh[0:n, i, :],
                                                    ALU.subtract).then_inc(job_lo, 1)
                        if j == MAX_AT[-1]:
                            whole_max(0)
                        if j == MAX_AT[-1] + 3:
                            make_shift(0)

                    def reciprocals(h, q):
                        if q == 0:
                            dve.wait_ge(den_mm, at(t, HALVES, h + 1))
                            dve.wait_ge(on_ok, at(t, HALVES, h))
                        nc.vector.reciprocal(rden[:, q * P:(q + 1) * P], dn[:, q * P:(q + 1) * P]).then_inc(rden_ok, 1)

                    def normalize(h):
                        dve.wait_ge(rden_ok, at(t, 4 * HALVES, 4 * h + 4))
                        dve.wait_ge(pv_mm, at(t, NT, (h + 1) * KT))
                        dve.wait_ge(wo_used, at(t, 4, h - 4 + 1))
                        nc.vector.tensor_tensor(ot[:, 2 * h:2 * h + 2, :], pv[:, h % 2, :].rearrange("p (g n) -> p g n", g=2),
                                                rden[:, :].rearrange("p (g n) -> p g n", g=2), ALU.mult).then_inc(on_ok, 1)

                    reduce_pair(1, 0)
                    for g in range(NT):
                        h, i = divmod(g, KT)
                        n = LAST if i == KT - 1 else P
                        h1, i1 = divmod(g + 1, KT)
                        if h1 + 1 < HALVES and i1 < PAIRS:
                            reduce_pair(h1 + 1, i1)
                        dve.wait_ge(hi_ok, at(t, NT, g + 1))
                        dve.wait_ge(pv_mm, at(t, NT, g - 1))
                        nc.vector.tensor_tensor(pl[0:n, g % 2, :], p32[0:n, g % 2, :], ph[0:n, g % 2, :],
                                                ALU.subtract).then_inc(lo_ok, 1)
                        if h + 1 < HALVES:
                            if i == PAIRS - 1:
                                whole_max(h + 1)
                            if i == PAIRS + 2:
                                make_shift(h + 1)
                        if h >= 1 and 8 <= i < 12:
                            reciprocals(h - 1, i - 8)
                        if h >= 1 and i == 12:
                            normalize(h - 1)
                    for q in range(4):
                        reciprocals(HALVES - 1, q)
                    normalize(HALVES - 1)
                    dve.wait_ge(wo_used, at(t, 4, 4))
                    for tb in range(TB):
                        res = nc.vector.tensor_tensor(xres[:, tb, :], xres[:, tb, :], mx[:, tb, :], ALU.add)
                        res.then_inc(xr_ok, 1)
                    dve.wait_ge(xr_ok, t * 2 + 2)
                    dve.sem_inc(mx_free, 1)
                all_meet(dve, b, 1)
                dve.wait_ge(f_ld, at(b, 64, 64))
                layernorm(b, 1, lambda tb: nc.vector.tensor_tensor(xres[:, tb, :], xres[:, tb, :], box[:, :], ALU.add))

                fv = [0]

                def step(ins):
                    ins.then_inc(f_v, 1)
                    fv[0] += 1

                def last():
                    dve.wait_ge(f_v, at(b, N_FV, fv[0]))
                dve.wait_ge(f_mm, at(b, TB, TB))
                step(nc.vector.tensor_copy(lg[:, :, :], mx[:, :, 0:NE]))
                last()
                held(dve)
                for tb in range(TB):
                    step(nc.vector.max(top8[:, tb, :], lg[:, tb, :]))
                last()
                held(dve)
                for tb in range(TB):
                    step(nc.vector.max_index(idx8[:, tb, :], top8[:, tb, :], lg[:, tb, :]))
                last()
                step(nc.vector.tensor_copy(idxf[:, :, :], idx8[:, :, :]))
                step(nc.vector.tensor_tensor(dv21[:, :], top8[:, :, 1], top8[:, :, 0], ALU.subtract))
                assert fv[0] == 7
                dve.wait_ge(f_e, at(b, 1, 1))
                step(nc.vector.tensor_scalar(den1[:, :], e21[:, :], 1.0, None, ALU.add))
                last()
                step(nc.vector.reciprocal(p1[:, :], den1[:, :]))
                last()
                step(nc.vector.tensor_scalar(p1s[:, :], p1[:, :], LORA_SCALING, None, ALU.mult))
                last()
                step(nc.vector.tensor_tensor(p2s[:, :], e21[:, :], p1s[:, :], ALU.mult))
                last()
                iota = cst[:, C_IOTA:C_IOTA + NE]
                for tb in range(TB):
                    for gk, ps, k in ((g1, p1s, 0), (g2, p2s, 1)):
                        step(nc.vector.tensor_scalar(gk[:, tb, :], iota, idxf[:, tb, k:k + 1], ps[:, tb:tb + 1],
                                                     ALU.is_equal, ALU.mult))
                last()
                step(nc.vector.tensor_tensor(gate[:, :, :], g1[:, :, :], g2[:, :, :], ALU.add))
                last()
                for tb in range(TB):
                    step(nc.vector.tensor_tensor(hg[:, tb, :].rearrange("p (e r) -> p e r", r=RANK),
                                                 mx[:, tb, NE:GA].rearrange("p (e r) -> p e r", r=RANK),
                                                 gate[:, tb, :].unsqueeze(2).broadcast_to([P, NE, RANK]), ALU.mult))
                assert fv[0] == N_FV, fv
                dve.wait_ge(f_o, at(b, TB, TB))
                layernorm(b, 2, lambda tb: nc.vector.tensor_tensor(xres[:, tb, :], xres[:, tb, :], bank[tb][:, :], ALU.add))
                all_meet(dve, b, 2)

        @block.tensor
        def _(pe):
            for s_, n in ((xt_ps, 4), (f_mm, TB), (f_t, TB), (f_o, TB), (s_qkv, 3), (s_sc, HB), (s_tp, HB), (s_pv, HB),
                          (s_y, 2), (wo_used, 4), (job, NJ), (mx_mm, HALVES * PAIRS), (mt_mm, HALVES), (sc_mm, NT),
                          (pv_mm, NT), (den_mm, HALVES)):
                pe.sem_inc(s_, n)
            pe.wait_ge(c_ld, N_CONST)
            pe.wait_ge(c_set, 8)

            def mm(dst, lhs, rhs, first, final):
                return nc.tensor.matmul(dst, lhs, rhs, start=first, stop=final)

            def transpose_x(b, k):
                pe.wait_ge(ln, at(b, 3 * N_LN, N_LN * (k + 1)))
                for tb in range(TB):
                    for c in range(DC):
                        tr = nc.tensor.transpose(bank[tb][:, c * P:(c + 1) * P], xres[:, tb, c * P:(c + 1) * P], ident)
                    tr.then_inc(xt_ps, 1)

            with pe.Fori(0, nb) as b:
                pe.wait_ge(x_ld, at(b, 64, 64))
                held(pe)
                with pe.Fori(0, NM) as m:
                    t = b * NM + m
                    pe.wait_ge(w_ld, at(t, 16, 16))
                    pe.wait_ge(s_res, at(t, 2, 0))
                    pe.wait_ge(s_rope, at(t, N_ROPE, 0))
                    for kind in range(4):
                        dst = bank[kind // 2][:, (kind % 2) * S:(kind % 2 + 1) * S]
                        for c in range(DC):
                            last = mm(dst, wsb[:, kind * 512 + c * P:kind * 512 + (c + 1) * P], xt[:, c, :], c == 0, c == DC - 1)
                        if kind % 2:
                            last.then_inc(s_qkv, 1)
                    for tb in range(TB):
                        for c in range(DC):
                            last = mm(bank[2][:, tb * P:(tb + 1) * P], xt[:, c, tb * P:(tb + 1) * P],
                                      wsb[:, 4 * 512 + c * P:4 * 512 + (c + 1) * P], c == 0, c == DC - 1)
                    last.then_inc(s_qkv, 1)
                    pe.wait_ge(s_rope, at(t, N_ROPE, 6))
                    pe.wait_ge(s_ot, at(t, 1, 0))
                    for h in range(HB + 3):
                        if h < HB:
                            sc = s_bank[h % 3]
                            pe.wait_ge(s_qm, at(t, HB, h + 1))
                            pe.wait_ge(s_exp, at(t, 2 * HB, 2 * h - 4))
                            if h == 2:
                                pe.wait_ge(s_rope, at(t, N_ROPE, N_ROPE))
                            for qb, a in ((0, 0), (1, 128)):
                                w = (qb + 1) * P
                                mm(sc[:, a:a + w], qm[:, h % 2, qb * P:(qb + 1) * P], kr[:, 0:w], True, False)
                                last = mm(sc[:, a + w - P:a + w], identb[:, :], maskb[:, :], False, True)
                            last.then_inc(s_sc, 1)
                        if 2 <= h < HB + 2:
                            k = h - 2
                            pe.wait_ge(s_pn, at(t, 2 * HB, 2 * k + 2))
                            pe.wait_ge(s_ptc, at(t, HB, k - 1))
                            for a in (0, 128, 256):
                                last = nc.tensor.transpose(pv[:, k % 2, a:a + P], pn[:, k % 3, a:a + P], ident)
                            last.then_inc(s_tp, 1)
                        if h >= 3:
                            k = h - 3
                            pe.wait_ge(s_ptc, at(t, HB, k + 1))
                            pe.wait_ge(s_rope, at(t, N_ROPE, N_ROPE))
                            mm(dn[:, 0:S], vx[:, 0, k * P:(k + 1) * P], pt[:, k % 2, 0:S], k == 0, False)
                            mm(dn[:, P:S], vx[:, 1, k * P:(k + 1) * P], pt[:, k % 2, S:S + P], False, k == HB - 1).then_inc(s_pv, 1)
                    pe.wait_ge(s_ot, at(t, 1, 1))
                    for tb in range(TB):
                        mm(bank[tb][:, :], ots[:, tb * P:(tb + 1) * P], wsb[:, 2560:3072], True, True).then_inc(s_y, 1)
                pe.wait_ge(s_res, at(b * NM + (NM - 1), 2, 2))
                transpose_x(b, 0)
                pe.wait_ge(split, at(b, N_STAGE, 5))
                pe.wait_ge(xt_ok, at(b, 4, 2))
                all_meet(pe, b, 0)
                with pe.Fori(0, NP) as p:
                    t = b * NP + p
                    pe.wait_ge(split, at(b, N_STAGE, 5) + p)

                    def max_pair(h, r):
                        kv, q0 = h // 2, (h % 2) * QH + (r // 2) * P
                        pe.wait_ge(mx_free, at(t, MXU, h * (PAIRS + 1) + r))
                        for half in range(2):
                            a, n = MCH[r % 2][half]
                            last = mm(mx[:, half, 0:n], qh[:, kv, q0:q0 + P], kh[:, kv, a:a + n], True, True)
                        last.then_inc(mx_mm, 1)

                    def transpose_max(h):
                        pe.wait_ge(m4_ok, at(t, HALVES, h + 1))
                        mm(mx[0:4, 0, 0:P], m4[:, h % 2, :], ident, True, True).then_inc(mt_mm, 1)

                    for j, (kind, kv, i) in enumerate(JOBS):
                        if j in MAX_AT:
                            if j == MAX_AT[0]:
                                pe.wait_ge(job_lo, at(t, NJ, 8))
                            max_pair(0, MAX_AT.index(j))
                        dst = bank[j % RING]
                        if j < RING:
                            pe.wait_ge(exp_ok, at(t, NT, j - RING + 1))
                        else:
                            pe.wait_ge(job_lo, at(t, NJ, j - RING + 1))
                        if kind == "K":
                            a, n = KCH[i]
                            w = slice(kv * P, (kv + 1) * P)
                            for c in range(DC):
                                mm(dst[:, 0:n], wkvh[:, c, w], ctxh[:, c, a:a + n], c == 0, False)
                                mm(dst[:, 0:n], wkvh[:, c, w], ctxl[:, c, a:a + n], False, False)
                                last = mm(dst[:, 0:n], wkvl[:, c, w], ctxh[:, c, a:a + n], False, c == DC - 1)
                        elif kind == "Q":
                            if i == 0:
                                pe.wait_ge(wq_ld, at(t, 32, 16 * (kv + 1)))
                            for c in range(DC):
                                last = mm(dst[:, 0:S], wqb[:, c, i * P:(i + 1) * P], xt[:, c, :], c == 0, c == DC - 1)
                        else:
                            n = LAST if i == KT - 1 else P
                            for c in range(DC):
                                keys = slice(i * P, i * P + n)
                                mm(dst[0:n, 0:256], ctxh[:, c, keys], wkvh[:, c, 256:512], c == 0, False)
                                mm(dst[0:n, 0:256], ctxh[:, c, keys], wkvl[:, c, 256:512], False, False)
                                last = mm(dst[0:n, 0:256], ctxl[:, c, keys], wkvh[:, c, 256:512], False, c == DC - 1)
                        last.then_inc(job, 1)
                        if j == MAX_AT[-1] + 2:
                            transpose_max(0)

                    def weigh(g):
                        h, i = divmod(g, KT)
                        kv, n = h // 2, LAST if i == KT - 1 else P
                        w = slice(kv * P, (kv + 1) * P)
                        if i == 0:
                            pe.wait_ge(on_ok, at(t, HALVES, h - 1))
                        pe.wait_ge(lo_ok, at(t, NT, g + 1))
                        dst = pv[:, h % 2, :]
                        mm(dst, vh[0:n, i, w], ph[0:n, g % 2, :], i == 0, False)
                        mm(dst, vh[0:n, i, w], pl[0:n, g % 2, :], False, False)
                        mm(dst, vl[0:n, i, w], ph[0:n, g % 2, :], False, i == KT - 1).then_inc(pv_mm, 1)

                    def denominators(h):
                        pe.wait_ge(sum_ok, at(t, HALVES * (KT - 1), (h + 1) * (KT - 1)))
                        pe.wait_ge(rden_ok, at(t, 4 * HALVES, 4 * h))
                        mm(dn[:, :], ones[:, :], psm[:, h % 2, :], True, True).then_inc(den_mm, 1)

                    for g in range(NT):
                        h, i = divmod(g, KT)
                        kv, q0 = h // 2, (h % 2) * QH
                        n = LAST if i == KT - 1 else P
                        keys, cols = slice(i * P, i * P + n), slice(q0, q0 + QH)
                        u = NJ + g
                        if h + 1 < HALVES and i < PAIRS:
                            max_pair(h + 1, i)
                        dst = bank[u % RING][0:n, :]
                        if g < RING:
                            pe.wait_ge(job_lo, at(t, NJ, NJ + g - RING + 1))
                        else:
                            pe.wait_ge(exp_ok, at(t, NT, g - RING + 1))
                        if g == 0:
                            pe.wait_ge(job_lo, at(t, NJ, NJ))
                        if i == 0:
                            pe.wait_ge(shift_ok, at(t, HALVES, h + 1))
                        mm(dst, kh[:, kv, keys], qh[:, kv, cols], True, False)
                        mm(dst, kh[:, kv, keys], ql[:, kv, cols], False, False)
                        mm(dst, kl[:, kv, keys], qh[:, kv, cols], False, False)
                        mm(dst, negones[:, 0:n], shift[:, h % 2, :, :].rearrange("p a c -> p (a c)"), False, True).then_inc(sc_mm, 1)
                        if g >= 2:
                            weigh(g - 2)
                        if h + 1 < HALVES and i == PAIRS + 1:
                            transpose_max(h + 1)
                        if h >= 1 and i == 3:
                            denominators(h - 1)
                    weigh(NT - 2)
                    weigh(NT - 1)
                    denominators(HALVES - 1)
                    pe.wait_ge(mx_free, at(t, MXU, MXU - 1))
                    for c in range(4):
                        pe.wait_ge(wo_ld[c % 2], at(t, 32, 16 * (c // 2 + 1)))
                        pe.wait_ge(ot_ok, at(t, HALVES, c + 1))
                        for k in range(2):
                            for tb in range(TB):
                                last = mm(mx[:, tb, :], ot[:, 2 * c + k, tb * P:(tb + 1) * P], wob[:, c % 2, k, :],
                                          c == 0 and k == 0, c == 3 and k == 1)
                        last.then_inc(wo_used, 1)
                all_meet(pe, b, 1)
                transpose_x(b, 1)
                pe.wait_ge(f_ld, at(b, 64, 64))
                pe.wait_ge(xt_ok, at(b, 4, 4))
                for tb in range(TB):
                    rows = slice(tb * P, (tb + 1) * P)
                    for c in range(DC):
                        last = mm(mx[:, tb, 0:GA], xt[:, c, rows], wgat[:, c, :], c == 0, c == DC - 1)
                    last.then_inc(f_mm, 1)
                for tb in range(TB):
                    for c in range(DC):
                        mm(bank[tb][:, :], xt[:, c, tb * P:(tb + 1) * P], wbt[:, c, :], c == 0, False)
                pe.wait_ge(f_v, at(b, N_FV, N_FV))
                for tb in range(TB):
                    for k, n in enumerate((P, ER - P)):
                        last = nc.tensor.transpose(pv[0:n, tb, k * P:(k + 1) * P], hg[:, tb, k * P:k * P + n], ident)
                    last.then_inc(f_t, 1)
                for tb in range(TB):
                    pe.wait_ge(f_tc, at(b, 4, 2 * tb + 2))
                    mm(bank[tb][:, :], hgt[:, tb, 0, :], wlbt[:, 0, :], False, False)
                    mm(bank[tb][:, :], hgt[0:ER - P, tb, 1, :], wlbt[0:ER - P, 1, :], False, True).then_inc(f_o, 1)
                all_meet(pe, b, 2)


_OUT = ((B, TB, P, D), "float32")


def kernel(**inputs):
    import concourse.bacc as bacc
    from concourse.bass_utils import run_bass_kernel_spmd

    nc = bacc.Bacc("TRN2", target_bir_lowering=False, num_devices=1)
    arrays = lay_out({k: np.asarray(v) for k, v in inputs.items()})
    args = {n: nc.dram_tensor(f"in_{n}", a.shape, mybir.dt.from_np(a.dtype), kind="ExternalInput").ap()
            for n, a in arrays.items()}
    o = nc.dram_tensor("out", (B, P, TB, D), F32, kind="ExternalOutput").ap()
    build(nc, **args, out=o)
    r = run_bass_kernel_spmd(nc, [{f"in_{n}": a for n, a in arrays.items()}], core_ids=[0])
    return np.ascontiguousarray(r.results[0]["out"].transpose(0, 2, 1, 3)).reshape(B, S, D)


def lay_out(i):
    c = np.ascontiguousarray
    swap = np.arange(D) ^ 1
    kinds = [(i["L0_attn_Wq"], i["L0_attn_bq"]), (i["L0_attn_Wq"][swap], i["L0_attn_bq"][swap]),
             (i["L0_attn_Wk"], i["L0_attn_bk"]), (i["L0_attn_Wk"][swap], i["L0_attn_bk"][swap]),
             (i["L0_attn_Wv"], i["L0_attn_bv"])]
    ws = np.zeros((NM, P, 3077), np.float32)
    for m in range(NM):
        rows = slice(m * P, (m + 1) * P)
        for k, (w, bias) in enumerate(kinds):
            ws[m, :, k * 512:(k + 1) * 512] = w[rows].T.reshape(DC, P, P).transpose(1, 0, 2).reshape(P, 512)
            ws[m, :, 3072 + k] = bias[rows]
        ws[m, :, 2560:3072] = i["L0_attn_Wo"].T[rows]
    w = i["L0_xattn_Wkv"].reshape(DC, P, 2, NP, 2 * XD).transpose(3, 1, 0, 2, 4).reshape(NP, P, DC * 4 * XD)
    wkv = c(np.concatenate([w, w[:1]]))
    wq = c(i["L0_xattn_Wq"].reshape(DC, P, XKV, G * XD).transpose(2, 1, 0, 3))
    wo = c(i["L0_xattn_Wo"].reshape(XH // 2, 2, P, D).transpose(0, 2, 1, 3))
    rows_b = lambda v: c(np.broadcast_to(v, (P, D)))
    wga = np.concatenate([i["L0_ffn_gate_W"], i["L0_ffn_lora_A"].reshape(ER, D)])
    wlb = np.zeros((2, P, D), np.float32)
    lb = i["L0_ffn_lora_B"].transpose(0, 2, 1).reshape(ER, D)
    wlb[0], wlb[1, :ER - P] = lb[:P], lb[P:]
    theta = (1.0 / 10000.0 ** (np.arange(0, DH, 2, dtype=np.float32) / DH)).astype(np.float32)
    ang = (np.arange(S, dtype=np.float32)[:, None] * theta[None, :]).astype(np.float32)
    d = np.arange(P) % DH
    sign = np.where(d % 2 == 0, -1.0, 1.0).astype(np.float32)
    rope = np.stack([np.cos(ang).T[d // 2], np.sin(ang).T[d // 2] * sign[:, None]], axis=1).astype(np.float32)
    consts = np.zeros((P, C_N), np.float32)
    consts[:, C_ID:C_ID + P] = np.eye(P)
    consts[:, C_HM:C_HM + HB] = np.arange(P)[:, None] // DH == np.arange(HB)
    consts[:, C_IOTA:C_IOTA + NE] = np.arange(NE)
    consts[:, C_EPS] = EPS
    consts[:, C_BK:C_BK + XKV] = i["L0_xattn_bkv"][:XKV * XD].reshape(XKV, XD).T
    consts[:, C_BV:C_BV + XKV] = i["L0_xattn_bkv"][XKV * XD:].reshape(XKV, XD).T
    consts[:, C_BQ:C_BQ + XH] = i["L0_xattn_bq"].reshape(XH, XD).T
    bmask = c(np.broadcast_to(np.eye(4, dtype=np.float32)[:, :, None], (4, 4, P)))
    return dict(
        x=c(i["x"].reshape(B, TB, P, D).transpose(0, 2, 1, 3)),
        x_t=c(i["x"].reshape(B, S, DC, P).transpose(0, 3, 2, 1)),
        ctx_t=c(i["ctx_4096"].reshape(B, LK, DC, P).transpose(0, 2, 3, 1)),
        ws=ws, wkv=wkv, wq=wq, wo=wo, bo_s=rows_b(i["L0_attn_bo"]), bo_x=rows_b(i["L0_xattn_bo"]),
        wb=c(i["L0_ffn_base_W"].T.reshape(DC, P, D).transpose(1, 0, 2)),
        wga=c(wga.T.reshape(DC, P, GA).transpose(1, 0, 2)), wlb=c(wlb.transpose(1, 0, 2)),
        rope=rope, consts=consts, bmask=bmask)
```

```python
from contextlib import ExitStack

import numpy as np

import concourse.bass as bass
from concourse import mybir

F32 = mybir.dt.float32
F32R = mybir.dt.float32r
BF16 = mybir.dt.bfloat16
U32 = mybir.dt.uint32
ALU = mybir.AluOpType
ACT = mybir.ActivationFunctionType
AX = mybir.AxisListType

P = 128
B, S, D = 4, 256, 512
DC = D // P
TB = S // P
NH, DH = 32, 16
HB = P // DH
NM = NH // HB
XH, XKV, XD = 32, 8, 128
G = XH // XKV
NP = XKV // 2
LK = 1601
KT = (LK + P - 1) // P
LAST = LK - (KT - 1) * P
LKP = LK + 1
NE, RANK = 28, 8
ER = NE * RANK
LORA_SCALING = 16 / 8
GA = NE + ER
EPS = 1e-5
NEG = -1.0e30
XSCALE = 1.0 / float(np.sqrt(XD))
SSCALE = 1.0 / float(np.sqrt(DH))

KCH = [(0, 400), (400, 400), (800, 400), (1200, 402)]
MCH = [((0, 400), (400, 400), 400), ((800, 402), (1200, 402), 401)]

PIECES = 4
CTX_PIECES = [(0, 400), (400, 800), (800, 1200), (1200, LK)]
WKV_AT = (3, 5, 7, 9)

JOBS = [("K", 0, j) for j in range(4)] + [("Q", 0, g) for g in range(G)] \
    + [("K", 1, j) for j in range(4)] + [("Q", 1, g) for g in range(G)] + [("V", 0, t) for t in range(KT)]
NJ = len(JOBS)
HALVES = 4
NT = HALVES * KT
QH = 2 * S
RING = 3
assert (NJ + NT) % RING == 0 and NT % 2 == 0
PAIRS = 8
MXU = HALVES * (PAIRS + 1) + 1
MAX_AT = (10, 12, 14, 16, 18, 20, 22, 24)
C_ID, C_HM, C_IOTA, C_EPS, C_BK, C_BV, C_BQ, C_SW = 0, 128, 136, 164, 165, 173, 181, 213
C_N = C_SW + P
W_QKV = 3 * D + 2


def at(turn, per_turn, n):
    return turn * per_turn + (per_turn + n)


def build(nc, x, x_t, ctx_t, ws, wkv, wq, wo, bo_s, bo_x, wb, wga, wlb, rope, consts, bmask, out, nb=B):
    with ExitStack() as ctx:
        def sb(name, shape, dt=F32, stack=ctx):
            return stack.enter_context(nc.sbuf_tensor(name, shape, dt))

        def sem(name):
            return ctx.enter_context(nc.semaphore(name))

        cst = sb("cst", [P, C_N])
        ones = sb("ones", [P, P])
        identb = sb("identb", [P, P], BF16)
        maskb = sb("maskb", [P, P], BF16)
        negones = sb("negones", [4, P], F32R)
        blockm = sb("blockm", [4, 4, P])
        xres = sb("xres", [P, TB, D])
        xt = sb("xt", [P, DC, S])
        stats = sb("stats", [P, TB, 6])
        mv = sb("mv", [P, TB, 2])
        rstd = sb("rstd", [P, TB])
        ctxh = sb("ctxh", [P, DC, LKP], F32R)
        ctxl = sb("ctxl", [P, DC, LKP], F32R)
        stage = sb("stage", [P, DC * 512])
        wkvh = sb("wkvh", [P, DC, 512], F32R)
        wkvl = sb("wkvl", [P, DC, 512], F32R)
        ident = cst[:, C_ID:C_ID + P]
        swap = cst[:, C_SW:C_SW + P]

        with ExitStack() as st:
            wbt = sb("wbt", [P, DC, D], stack=st)
            wgat = sb("wgat", [P, DC, GA], stack=st)
            wlbt = sb("wlbt", [P, 2, D], stack=st)
            box = sb("box", [P, D], stack=st)
            lg = sb("lg", [P, TB, NE], stack=st)
            top8 = sb("top8", [P, TB, 8], stack=st)
            idx8 = sb("idx8", [P, TB, 8], U32, stack=st)
            idxf = sb("idxf", [P, TB, 8], stack=st)
            dv21 = sb("dv21", [P, TB], stack=st)
            e21 = sb("e21", [P, TB], stack=st)
            den1 = sb("den1", [P, TB], stack=st)
            p1 = sb("p1", [P, TB], stack=st)
            p1s = sb("p1s", [P, TB], stack=st)
            p2s = sb("p2s", [P, TB], stack=st)
            g1 = sb("g1", [P, TB, NE], stack=st)
            g2 = sb("g2", [P, TB, NE], stack=st)
            gate = sb("gate", [P, TB, NE], stack=st)
            hg = sb("hg", [P, TB, ER], stack=st)
            hgt = sb("hgt", [P, TB, 2, P], stack=st)
            wqkv = sb("wqkv", [P, W_QKV], stack=st)
            wos = sb("wos", [P, D + 1], stack=st)
            qkb = sb("qkb", [P, 2, S], stack=st)
            rp = sb("rp", [P, 2, S], stack=st)
            bos = sb("bos", [P, D], stack=st)
            qr = sb("qr", [P, S], stack=st)
            kr = sb("kr", [P, S], stack=st)
            t1 = sb("t1", [P, S], stack=st)
            t2 = sb("t2", [P, S], stack=st)
            qm = sb("qm", [P, 2, S], stack=st)
            vx = sb("vx", [P, TB, HB * (P + DH)], stack=st)
            pn = sb("pn", [P, 3, 384], stack=st)
            pt = sb("pt", [P, 2, 384], stack=st)
            nmx = sb("nmx", [P, 3, 2], stack=st)
            sm = sb("sm", [P, 3, 2], stack=st)
            rsm = sb("rsm", [P, 3, 2], stack=st)
            ots = sb("ots", [P, S], stack=st)
        kh = sb("kh", [P, 2, LKP], F32R)
        kl = sb("kl", [P, 2, LKP], F32R)
        vh = sb("vh", [P, KT, 256], F32R)
        vl = sb("vl", [P, KT, 256], F32R)
        qh = sb("qh", [P, 2, G * S], F32R)
        ql = sb("ql", [P, 2, G * S], F32R)
        wqb = sb("wqb", [P, DC, G * XD])
        wob = sb("wob", [P, 2, 2, D])
        p32 = sb("p32", [P, 2, QH])
        ph = sb("ph", [P, 2, QH], F32R)
        pl = sb("pl", [P, 2, QH], F32R)
        psm = sb("psm", [P, 2, QH])
        rden = sb("rden", [P, QH])
        ot = sb("ot", [P, 2 * G, S])
        shift = sb("shift", [4, 2, 4, P], F32R)
        mxp = sb("mxp", [P, 2, PAIRS])
        m4 = sb("m4", [P, 2, 4])

        bank = [ctx.enter_context(nc.psum_tensor(f"bank{i}", [P, 512], F32)) for i in range(RING)]
        mx = ctx.enter_context(nc.psum_tensor("mx", [P, 2, 512], F32))
        pv = ctx.enter_context(nc.psum_tensor("pv", [P, 2, 512], F32))
        dn = ctx.enter_context(nc.psum_tensor("dn", [P, 512], F32))
        s_bank = [mx[:, 0, :], mx[:, 1, :], bank[2][:, :]]

        c_ld, c_set, phase, passed = (sem(n) for n in ("c_ld", "c_set", "phase", "passed"))
        x_ld, xt_ld, rp_ld, f_ld, stage_ld, split, stored = (sem(n) for n in ("x_ld", "xt_ld", "rp_ld", "f_ld", "stage_ld", "split", "stored"))
        split_hi, split_lo, xr_ok = sem("split_hi"), sem("split_lo"), sem("xr_ok")
        ln, ln_sd, xt_ps, xt_ok = (sem(n) for n in ("ln", "ln_sd", "xt_ps", "xt_ok"))
        f_mm, f_base, f_v, f_e, f_t, f_tc, f_o = (sem(n) for n in ("f_mm", "f_base", "f_v", "f_e", "f_t", "f_tc", "f_o"))
        wq1_ld, wo1_ld, s_qkv, s_qkb, s_rope, s_vz = (sem(n) for n in ("wq1_ld", "wo1_ld", "s_qkv", "s_qkb", "s_rope", "s_vz"))
        s_qm, s_sc, s_mx, s_exp, s_rs, s_pn = (sem(n) for n in ("s_qm", "s_sc", "s_mx", "s_exp", "s_rs", "s_pn"))
        s_tp, s_ptc, s_pv, s_ot, s_y, s_res = (sem(n) for n in ("s_tp", "s_ptc", "s_pv", "s_ot", "s_y", "s_res"))
        wq_ld, wo_ld, wo_used = sem("wq_ld"), [sem("wo_ld0"), sem("wo_ld1")], sem("wo_used")
        job, job_hi, job_lo = sem("job"), sem("job_hi"), sem("job_lo")
        mx_mm, mx_free, m4_ok, mt_mm, shift_ok = (sem(n) for n in ("mx_mm", "mx_free", "m4_ok", "mt_mm", "shift_ok"))
        sc_mm, exp_ok, hi_ok, lo_ok, sum_ok, pv_mm = (sem(n) for n in ("sc_mm", "exp_ok", "hi_ok", "lo_ok", "sum_ok", "pv_mm"))
        den_mm, rden_ok, on_ok, ot_ok = (sem(n) for n in ("den_mm", "rden_ok", "on_ok", "ot_ok"))

        N_STAGE = 4 + NP
        N_CONST = 2 * 16
        N_ROPE = 8
        N_LN = 9
        N_FV = 7 + 4 + 2 * TB + 1 + TB

        def held(eng):
            eng.sem_inc(passed, 1)

        block = ctx.enter_context(nc.Block())

        @block.sync
        def _(sp):
            sp.dma_start(cst[:, :], consts).then_inc(c_ld, 16)
            sp.dma_start(blockm[:, :, :], bmask).then_inc(c_ld, 16)
            for s_, n in ((x_ld, 32), (xt_ld, 16), (rp_ld, 16), (f_ld, 64), (stage_ld, 16 * N_STAGE),
                          (wq1_ld, 16), (wo1_ld, 16), (wq_ld, 32), (wo_ld[0], 32), (wo_ld[1], 32), (stored, 16)):
                sp.sem_inc(s_, n)

            def first_weights():
                sp.dma_start(wqkv[:, :], ws[0, :, 0:W_QKV]).then_inc(wq1_ld, 16)
                sp.dma_start(rp[:, :, :], rope).then_inc(rp_ld, 16)
                sp.dma_start(wos[:, :], ws[0, :, W_QKV:W_QKV + D + 1]).then_inc(wo1_ld, 16)
                sp.dma_start(bos[:, :], bo_s).then_inc(x_ld, 16)

            sp.dma_start(xt[:, :, :], x_t[0]).then_inc(xt_ld, 16)
            first_weights()
            sp.dma_start(xres[:, :, :], x[0]).then_inc(x_ld, 16)
            sp.dma_start(stage[:, :], wkv[0]).then_inc(stage_ld, 16)
            with sp.Fori(0, nb) as b:
                with sp.Fori(0, NM - 1) as m:
                    t = b * NM + m
                    sp.wait_ge(split, at(b, N_STAGE, 1) + m)
                    held(sp)
                    sp.dma_start(stage[:, 0:LK], ctx_t[b, m]).then_inc(stage_ld, 16)
                    sp.wait_ge(s_qkv, at(t, 5, 5))
                    held(sp)
                    sp.wait_ge(s_qkb, at(t, 2, 2))
                    held(sp)
                    sp.dma_start(wqkv[:, :], ws[m + 1, :, 0:W_QKV]).then_inc(wq1_ld, 16)
                    sp.wait_ge(s_y, at(t, 2, 2))
                    held(sp)
                    sp.dma_start(wos[:, :], ws[m + 1, :, W_QKV:W_QKV + D + 1]).then_inc(wo1_ld, 16)
                sp.wait_ge(split, at(b, N_STAGE, NM))
                sp.dma_start(stage[:, 0:LK], ctx_t[b, NM - 1]).then_inc(stage_ld, 16)
                sp.wait_ge(xt_ps, at(b, 4, 2))
                held(sp)
                with sp.Fori(0, NP) as p:
                    t = b * NP + p
                    for kv in range(2):
                        sp.wait_ge(job, at(t, NJ, 0) if kv == 0 else at(t, NJ, 8))
                        sp.dma_start(wqb[:, :, :], wq[2 * p + kv]).then_inc(wq_ld, 16)
                    sp.wait_ge(split, at(b, N_STAGE, 5) + p)
                    sp.dma_start(stage[:, :], wkv[p + 1]).then_inc(stage_ld, 16)
                    for c in range(4):
                        sp.wait_ge(wo_used, at(t, 4, c - 1))
                        sp.dma_start(wob[:, c % 2, :, :], wo[4 * p + c]).then_inc(wo_ld[c % 2], 16)
                sp.wait_ge(sc_mm, at(b * NP + (NP - 1), NT, NT))
                held(sp)
                sp.dma_start(box[:, :], bo_x).then_inc(f_ld, 16)
                sp.dma_start(wgat[:, :, :], wga).then_inc(f_ld, 16)
                sp.dma_start(wbt[:, :, :], wb).then_inc(f_ld, 16)
                sp.dma_start(wlbt[:, :, :], wlb).then_inc(f_ld, 16)
                sp.wait_ge(wo_used, at(b * NP + (NP - 1), 4, 4))
                held(sp)
                first_weights()
                sp.wait_ge(f_base, at(b, 1, 1))
                held(sp)
                sp.dma_start(xt[:, :, :], x_t[b + 1]).then_inc(xt_ld, 16)
                sp.wait_ge(ln, at(b, 3 * N_LN, 3 * N_LN))
                held(sp)
                sp.dma_start(out[b], xres[:, :, :]).then_inc(stored, 16)
                sp.wait_ge(stored, at(b, 16, 16))
                held(sp)
                sp.dma_start(xres[:, :, :], x[b + 1]).then_inc(x_ld, 16)
            for load, primed, in_sequence in ((x_ld, 32, 32), (xt_ld, 16, 16), (rp_ld, 16, 16), (wq1_ld, 16, 16 * NM),
                                              (wo1_ld, 16, 16 * NM), (stage_ld, 16 * N_STAGE, 16 * N_STAGE)):
                sp.wait_ge(load, primed + nb * in_sequence + (32 if load is x_ld else 16))

        @block.gpsimd
        def _(pool):
            nc.gpsimd.memset(ones[:, :], 1.0).then_inc(c_set, 1)
            nc.gpsimd.memset(negones[:, :].bitcast(F32), -1.0).then_inc(c_set, 1)
            nc.gpsimd.memset(ctxh[:, :, LK:LKP].bitcast(F32), 0.0).then_inc(c_set, 1)
            nc.gpsimd.memset(ctxl[:, :, LK:LKP].bitcast(F32), 0.0).then_inc(c_set, 1)
            nc.gpsimd.memset(identb[:, :], 0.0).then_inc(c_set, 1)
            nc.gpsimd.memset(maskb[:, :], 0.0).then_inc(c_set, 1)
            pool.wait_ge(c_set, 6)
            nc.gpsimd.affine_select(out=identb[:, :], in_=identb[:, :], compare_op=ALU.not_equal, fill=1.0,
                                    base=0, pattern=[[-1, P]], channel_multiplier=1).then_inc(c_set, 1)
            nc.gpsimd.affine_select(out=maskb[:, :], in_=maskb[:, :], compare_op=ALU.is_ge, fill=NEG,
                                    base=0, pattern=[[-1, P]], channel_multiplier=1).then_inc(c_set, 1)
            pool.sem_inc(split, N_STAGE)
            pool.sem_inc(sum_ok, HALVES * (KT - 1))
            nc.gpsimd.memset(vx[:, :, :], 0.0).then_inc(s_vz, 1)
            wstage = stage[:, :].rearrange("p (c n) -> p c n", c=DC)

            def low_part(k, lo, hi, src, n):
                pool.wait_ge(split_hi, n * PIECES + k + 1)
                part = nc.gpsimd.tensor_tensor(lo, src, hi, ALU.subtract)
                part.then_inc(split_lo, 1)
                if k == PIECES - 1:
                    pool.wait_ge(split_lo, (n + 1) * PIECES)
                    pool.sem_inc(split, 1)

            for k in range(PIECES):
                low_part(k, wkvl[:, k, :], wkvh[:, k, :], wstage[:, k, :], 0)
            with pool.Fori(0, nb) as b:
                with pool.Fori(0, DC) as c:
                    for k, (a, z) in enumerate(CTX_PIECES):
                        low_part(k, ctxl[:, c, a:z], ctxh[:, c, a:z], stage[:, a:z], b * N_STAGE + c + 1)
                with pool.Fori(0, NP) as p:
                    t = b * NP + p
                    for h in range(HALVES):
                        acc = psm[:, h % 2, :]
                        pool.wait_ge(den_mm, at(t, HALVES, h - 1))
                        for i in range(1, KT):
                            n = LAST if i == KT - 1 else P
                            g = h * KT + i
                            pool.wait_ge(exp_ok, at(t, NT, g + 1))
                            if i == 1:
                                add = nc.gpsimd.tensor_tensor(acc, p32[:, (g - 1) % 2, :], p32[:, g % 2, :], ALU.add)
                            else:
                                pool.wait_ge(sum_ok, at(t, HALVES * (KT - 1), h * (KT - 1) + i - 1))
                                add = nc.gpsimd.tensor_tensor(acc[0:n], acc[0:n], p32[0:n, g % 2, :], ALU.add)
                            add.then_inc(sum_ok, 1)
                            if h == 1 and i in WKV_AT:
                                k = WKV_AT.index(i)
                                low_part(k, wkvl[:, k, :], wkvh[:, k, :], wstage[:, k, :], b * N_STAGE + 5 + p)
                pool.wait_ge(wo_used, at(b * NP + (NP - 1), 4, 4))
                held(pool)
                nc.gpsimd.memset(vx[:, :, :], 0.0).then_inc(s_vz, 1)

        def sums_after(g):
            h, i = divmod(g, KT)
            return h * (KT - 1) + max(i, 1)

        def add_bv(act, t, p, h):
            act.wait_ge(on_ok, at(t, HALVES, h + 1))
            held(act)
            nc.scalar.activation(ot[:, 2 * h:2 * h + 2, :], ot[:, 2 * h:2 * h + 2, :], ACT.Identity,
                                 bias=cst[:, bass.ds(2 * p + (C_BV + h // 2), 1)]).then_inc(ot_ok, 1)

        @block.scalar
        def _(act):
            for s_, n in ((ln_sd, 3), (xt_ok, 4), (f_e, 1), (f_tc, 4), (s_exp, 2 * HB), (s_ptc, HB), (s_ot, 1), (s_qkb, 2),
                          (job_hi, NJ), (exp_ok, NT), (hi_ok, NT), (ot_ok, HALVES)):
                act.sem_inc(s_, n)
            act.wait_ge(c_ld, N_CONST)

            def deviation(b, k):
                act.wait_ge(ln, at(b, 3 * N_LN, N_LN * k + 6))
                nc.scalar.activation(rstd[:, :], mv[:, :, 1], ACT.Sqrt, bias=cst[:, C_EPS:C_EPS + 1]).then_inc(ln_sd, 1)

            def copy_xt(b, k):
                for tb in range(TB):
                    act.wait_ge(xt_ps, at(b, 2 * TB, TB * k + tb + 1))
                    nc.scalar.activation(xt[:, :, tb * P:(tb + 1) * P],
                                         bank[tb][:, :].rearrange("p (c n) -> p c n", c=DC), ACT.Copy).then_inc(xt_ok, 1)

            def high_part(hi, src):
                nc.scalar.activation(hi, src, ACT.Copy).then_inc(split_hi, 1)

            wstage = stage[:, :].rearrange("p (c n) -> p c n", c=DC)
            act.wait_ge(stage_ld, 16 * N_STAGE + 16)
            for k in range(PIECES):
                high_part(wkvh[:, k, :], wstage[:, k, :])

            with act.Fori(0, nb) as b:
                with act.Fori(0, NM) as m:
                    t = b * NM + m
                    act.wait_ge(wq1_ld, at(t, 16, 16))
                    for k in range(2):
                        act.wait_ge(s_qkv, at(t, 5, k + 1))
                        act.wait_ge(s_rope, at(t, N_ROPE, 3 * k - 2))
                        nc.scalar.activation(qkb[:, k, :], bank[k][:, 0:S],
                                             ACT.Identity, bias=wqkv[:, 3 * D + k:3 * D + k + 1]).then_inc(s_qkb, 1)
                    act.wait_ge(s_y, at(t, 2, 0))
                    for h in range(HB + 2):
                        if h < HB:
                            act.wait_ge(s_mx, at(t, 2 * HB, 2 * h + 2))
                            act.wait_ge(s_tp, at(t, HB, h - 2))
                            act.wait_ge(s_rs, at(t, HB, h - 2))
                            for qb, (a, z) in enumerate(((0, 128), (128, 384))):
                                nc.scalar.activation(pn[:, h % 3, a:z], s_bank[h % 3][:, a:z], ACT.Exp,
                                                     bias=nmx[:, h % 3, qb:qb + 1],
                                                     accum_out=sm[:, h % 3, qb:qb + 1]).then_inc(s_exp, 1)
                        if h >= 2:
                            k = h - 2
                            act.wait_ge(s_tp, at(t, HB, k + 1))
                            act.wait_ge(s_pv, at(t, HB, k - 1))
                            nc.scalar.activation(pt[:, k % 2, :], pv[:, k % 2, 0:384], ACT.Copy).then_inc(s_ptc, 1)
                        if h in (1, 3, 5, 7):
                            if h == 1:
                                act.wait_ge(stage_ld, 16 * (b * N_STAGE + m) + 16 * (N_STAGE + 2))
                                held(act)
                            a, z = CTX_PIECES[h // 2]
                            high_part(ctxh[:, bass.ds(m, 1), a:z], stage[:, a:z].unsqueeze(1))
                    act.wait_ge(s_pv, at(t, HB, HB))
                    act.wait_ge(wo1_ld, at(t, 16, 16))
                    nc.scalar.activation(ots[:, :], dn[:, 0:S], ACT.Identity, bias=wos[:, D:D + 1]).then_inc(s_ot, 1)
                deviation(b, 0)
                copy_xt(b, 0)
                with act.Fori(0, NP) as p:
                    t = b * NP + p
                    for j, (kind, kv, i) in enumerate(JOBS):
                        act.wait_ge(job, at(t, NJ, j + 1))
                        src = bank[j % RING]
                        if kind == "K":
                            a, n = KCH[i]
                            if i == 0 and kv == 0:
                                act.wait_ge(sc_mm, at(t, NT, 0))
                            held(act)
                            nc.scalar.activation(kh[:, kv, a:a + n], src[:, 0:n], ACT.Identity,
                                                 bias=cst[:, bass.ds(2 * p + (C_BK + kv), 1)]).then_inc(job_hi, 1)
                        elif kind == "Q":
                            held(act)
                            nc.scalar.activation(qh[:, kv, i * S:(i + 1) * S], src[:, 0:S], ACT.Identity,
                                                 bias=cst[:, bass.ds(8 * p + (C_BQ + G * kv + i), 1)]).then_inc(job_hi, 1)
                        else:
                            n = LAST if i == KT - 1 else P
                            if i == 0:
                                act.wait_ge(pv_mm, at(t, NT, 0))
                            nc.scalar.activation(vh[0:n, i, :], src[0:n, 0:256], ACT.Copy).then_inc(job_hi, 1)
                    for g in range(NT):
                        h, i = divmod(g, KT)
                        n = LAST if i == KT - 1 else P
                        act.wait_ge(sc_mm, at(t, NT, g + 1))
                        act.wait_ge(sum_ok, at(t, HALVES * (KT - 1), sums_after(g - 2)))
                        act.wait_ge(lo_ok, at(t, NT, g - 1))
                        nc.scalar.activation(p32[0:n, g % 2, :], bank[(NJ + g) % RING][0:n, :], ACT.Exp,
                                             scale=XSCALE).then_inc(exp_ok, 1)
                        act.wait_ge(exp_ok, at(t, NT, g + 1))
                        act.wait_ge(pv_mm, at(t, NT, g - 1))
                        nc.scalar.activation(ph[0:n, g % 2, :], p32[0:n, g % 2, :], ACT.Copy).then_inc(hi_ok, 1)
                        if h == 1 and i in WKV_AT:
                            k = WKV_AT.index(i)
                            if k == 0:
                                act.wait_ge(stage_ld, 16 * (b * N_STAGE + p) + 16 * (N_STAGE + 6))
                                act.wait_ge(job, at(t, NJ, NJ))
                            high_part(wkvh[:, k, :], wstage[:, k, :])
                        if i == KT - 1 and h >= 1:
                            add_bv(act, t, p, h - 1)
                    add_bv(act, t, p, HALVES - 1)
                deviation(b, 1)
                copy_xt(b, 1)
                act.wait_ge(f_v, at(b, N_FV, 7))
                nc.scalar.activation(e21[:, :], dv21[:, :], ACT.Exp).then_inc(f_e, 1)
                for tb in range(TB):
                    act.wait_ge(f_t, at(b, TB, tb + 1))
                    for k, n in enumerate((P, ER - P)):
                        nc.scalar.activation(hgt[0:n, tb, k, :], pv[0:n, tb, k * P:(k + 1) * P], ACT.Copy).then_inc(f_tc, 1)
                deviation(b, 2)

        @block.vector
        def _(dve):
            for s_, n in ((ln, 3 * N_LN), (f_v, N_FV), (s_rope, N_ROPE), (s_qm, HB), (s_mx, 2 * HB), (s_rs, HB),
                          (s_pn, 2 * HB), (s_res, 2), (job_lo, NJ), (mx_free, MXU), (m4_ok, HALVES),
                          (shift_ok, HALVES), (lo_ok, NT), (rden_ok, 4 * HALVES), (on_ok, HALVES)):
                dve.sem_inc(s_, n)
            dve.wait_ge(c_ld, N_CONST)

            def layernorm(b, k, add):
                def done(n):
                    dve.wait_ge(ln, at(b, 3 * N_LN, N_LN * k + n))
                for tb in range(TB):
                    add(tb).then_inc(ln, 1)
                done(2)
                for tb in range(TB):
                    nc.vector.bn_stats(stats[:, tb, :], xres[:, tb, :]).then_inc(ln, 1)
                done(4)
                held(dve)
                for tb in range(TB):
                    nc.vector.bn_aggr(mv[:, tb, :], stats[:, tb, :]).then_inc(ln, 1)
                dve.wait_ge(ln_sd, at(b, 3, k + 1))
                nc.vector.reciprocal(rstd[:, :], rstd[:, :]).then_inc(ln, 1)
                done(7)
                for tb in range(TB):
                    nc.vector.tensor_scalar(xres[:, tb, :], xres[:, tb, :], mv[:, tb, 0:1], rstd[:, tb:tb + 1],
                                            ALU.subtract, ALU.mult).then_inc(ln, 1)

            with dve.Fori(0, nb) as b:
                dve.wait_ge(s_vz, b + 1)
                held(dve)
                dve.wait_ge(rp_ld, at(b, 16, 16))
                held(dve)
                with dve.Fori(0, NM) as m:
                    t = b * NM + m
                    for k, dst in enumerate((qr, kr)):
                        if k == 0:
                            dve.wait_ge(s_rope, at(t, N_ROPE, 0))
                            dve.wait_ge(s_qm, at(t, HB, 0))
                        else:
                            dve.wait_ge(s_rope, at(t, N_ROPE, 3))
                            dve.wait_ge(s_sc, at(t, HB, 0))
                        dve.wait_ge(s_qkb, at(t, 2, k + 1))
                        nc.vector.tensor_tensor(t1[:, :], qkb[:, k, :], rp[:, 0, :], ALU.mult).then_inc(s_rope, 1)
                        dve.wait_ge(s_qkv, at(t, 5, 4 + k))
                        nc.vector.tensor_tensor(t2[:, :], bank[k][:, S:2 * S], rp[:, 1, :], ALU.mult).then_inc(s_rope, 1)
                        dve.wait_ge(s_rope, at(t, N_ROPE, 3 * k + 2))
                        nc.vector.tensor_tensor(dst[:, :], t1[:, :], t2[:, :], ALU.add).then_inc(s_rope, 1)
                    dve.wait_ge(s_qkv, at(t, 5, 3))
                    dve.wait_ge(s_pv, at(t, HB, 0))
                    for tb in range(TB):
                        nc.vector.tensor_copy(vx[:, tb, :].rearrange("p (h x) -> p h x", h=HB)[:, :, 0:DH],
                                              bank[2][:, tb * P:(tb + 1) * P].rearrange("p (h x) -> p h x", h=HB)).then_inc(s_rope, 1)
                    dve.wait_ge(s_rope, at(t, N_ROPE, 3))

                    def one_head(h):
                        dve.wait_ge(s_sc, at(t, HB, h - 1))
                        nc.vector.tensor_scalar(qm[:, h % 2, :], qr[:, :], cst[:, C_HM + h:C_HM + h + 1], SSCALE,
                                                ALU.mult, ALU.mult).then_inc(s_qm, 1)
                    one_head(0)
                    one_head(1)
                    for h in range(HB + 1):
                        if h < HB:
                            dve.wait_ge(s_sc, at(t, HB, h + 1))
                            dve.wait_ge(s_exp, at(t, 2 * HB, 2 * h - 4))
                            for qb, (a, z) in enumerate(((0, 128), (128, 384))):
                                nc.vector.tensor_reduce(nmx[:, h % 3, qb:qb + 1], s_bank[h % 3][:, a:z], AX.X, ALU.max,
                                                        negate=True).then_inc(s_mx, 1)
                        if h + 2 < HB:
                            one_head(h + 2)
                        if h >= 1:
                            k = h - 1
                            dve.wait_ge(s_exp, at(t, 2 * HB, 2 * k + 2))
                            dve.wait_ge(s_pn, at(t, 2 * HB, 2 * k - 4))
                            nc.vector.reciprocal(rsm[:, k % 3, :], sm[:, k % 3, :]).then_inc(s_rs, 1)
                            dve.wait_ge(s_rs, at(t, HB, k + 1))
                            for qb, (a, z) in enumerate(((0, 128), (128, 384))):
                                nc.vector.tensor_scalar(pn[:, k % 3, a:z], pn[:, k % 3, a:z], rsm[:, k % 3, qb:qb + 1],
                                                        None, ALU.mult).then_inc(s_pn, 1)
                    dve.wait_ge(x_ld, at(b, 32, 32))
                    for tb in range(TB):
                        dve.wait_ge(s_y, at(t, 2, tb + 1))
                        dve.wait_ge(s_res, at(t, 2, tb - 1))
                        nc.vector.tensor_tensor(xres[:, tb, :], xres[:, tb, :], bank[tb][:, :], ALU.add).then_inc(s_res, 1)
                dve.wait_ge(s_res, at(b * NM + (NM - 1), 2, 2))
                layernorm(b, 0, lambda tb: nc.vector.tensor_tensor(xres[:, tb, :], xres[:, tb, :], bos[:, :], ALU.add))
                with dve.Fori(0, NP) as p:
                    t = b * NP + p

                    def reduce_pair(h, r):
                        k = h * (PAIRS + 1) + r
                        n = MCH[r % 2][2]
                        dve.wait_ge(mx_mm, at(t, HALVES * PAIRS, h * PAIRS + r + 1))
                        if r == 0:
                            dve.wait_ge(m4_ok, at(t, HALVES, h - 1))
                        nc.vector.tensor_reduce(mxp[:, h % 2, r:r + 1], mx[:, :, 0:n], AX.XY, ALU.max).then_inc(mx_free, 1)
                        assert k < MXU

                    def whole_max(h):
                        dve.wait_ge(mx_free, at(t, MXU, h * (PAIRS + 1) + PAIRS))
                        dve.wait_ge(mt_mm, at(t, HALVES, h - 1))
                        nc.vector.tensor_reduce(m4[:, h % 2, :], mxp[:, h % 2, :].rearrange("p (a c) -> p a c", c=2),
                                                AX.X, ALU.max).then_inc(m4_ok, 1)

                    def make_shift(h):
                        dve.wait_ge(mt_mm, at(t, HALVES, h + 1))
                        dve.wait_ge(sc_mm, at(t, NT, (h - 1) * KT))
                        nc.vector.tensor_tensor(shift[:, h % 2, :, :], blockm[:, :, :],
                                                mx[0:4, 0:1, 0:P].broadcast_to([4, 4, P]), ALU.mult).then_inc(shift_ok, 1)
                        dve.wait_ge(shift_ok, at(t, HALVES, h + 1))
                        dve.sem_inc(mx_free, 1)

                    for j, (kind, kv, i) in enumerate(JOBS):
                        if j in MAX_AT:
                            reduce_pair(0, MAX_AT.index(j))
                        dve.wait_ge(job_hi, at(t, NJ, j + 1))
                        src = bank[j % RING]
                        if kind == "K":
                            a, n = KCH[i]
                            nc.vector.scalar_tensor_tensor(kl[:, kv, a:a + n], src[:, 0:n],
                                                           cst[:, bass.ds(2 * p + (C_BK + kv), 1)],
                                                           kh[:, kv, a:a + n], ALU.add, ALU.subtract).then_inc(job_lo, 1)
                        elif kind == "Q":
                            nc.vector.scalar_tensor_tensor(ql[:, kv, i * S:(i + 1) * S], src[:, 0:S],
                                                           cst[:, bass.ds(8 * p + (C_BQ + G * kv + i), 1)],
                                                           qh[:, kv, i * S:(i + 1) * S], ALU.add, ALU.subtract).then_inc(job_lo, 1)
                        else:
                            n = LAST if i == KT - 1 else P
                            nc.vector.tensor_tensor(vl[0:n, i, :], src[0:n, 0:256], vh[0:n, i, :],
                                                    ALU.subtract).then_inc(job_lo, 1)
                        if j == MAX_AT[-1]:
                            whole_max(0)
                        if j == MAX_AT[-1] + 3:
                            make_shift(0)

                    def reciprocals(h, q):
                        if q == 0:
                            dve.wait_ge(den_mm, at(t, HALVES, h + 1))
                            dve.wait_ge(on_ok, at(t, HALVES, h))
                        nc.vector.reciprocal(rden[:, q * P:(q + 1) * P], dn[:, q * P:(q + 1) * P]).then_inc(rden_ok, 1)

                    def normalize(h):
                        dve.wait_ge(rden_ok, at(t, 4 * HALVES, 4 * h + 4))
                        dve.wait_ge(pv_mm, at(t, NT, (h + 1) * KT))
                        dve.wait_ge(wo_used, at(t, 4, h - 4 + 1))
                        nc.vector.tensor_tensor(ot[:, 2 * h:2 * h + 2, :], pv[:, h % 2, :].rearrange("p (g n) -> p g n", g=2),
                                                rden[:, :].rearrange("p (g n) -> p g n", g=2), ALU.mult).then_inc(on_ok, 1)

                    reduce_pair(1, 0)
                    for g in range(NT):
                        h, i = divmod(g, KT)
                        n = LAST if i == KT - 1 else P
                        h1, i1 = divmod(g + 1, KT)
                        if h1 + 1 < HALVES and i1 < PAIRS:
                            reduce_pair(h1 + 1, i1)
                        dve.wait_ge(hi_ok, at(t, NT, g + 1))
                        dve.wait_ge(pv_mm, at(t, NT, g - 1))
                        nc.vector.tensor_tensor(pl[0:n, g % 2, :], p32[0:n, g % 2, :], ph[0:n, g % 2, :],
                                                ALU.subtract).then_inc(lo_ok, 1)
                        if h + 1 < HALVES:
                            if i == PAIRS - 1:
                                whole_max(h + 1)
                            if i == PAIRS + 2:
                                make_shift(h + 1)
                        if h >= 1 and 7 <= i < 11:
                            reciprocals(h - 1, i - 7)
                        if h >= 1 and i == 11:
                            normalize(h - 1)
                    for q in range(4):
                        reciprocals(HALVES - 1, q)
                    normalize(HALVES - 1)
                    dve.wait_ge(wo_used, at(t, 4, 4))
                    for tb in range(TB):
                        res = nc.vector.tensor_tensor(xres[:, tb, :], xres[:, tb, :], mx[:, tb, :], ALU.add)
                        res.then_inc(xr_ok, 1)
                    dve.wait_ge(xr_ok, t * 2 + 2)
                    dve.sem_inc(mx_free, 1)
                dve.wait_ge(f_ld, at(b, 64, 64))
                layernorm(b, 1, lambda tb: nc.vector.tensor_tensor(xres[:, tb, :], xres[:, tb, :], box[:, :], ALU.add))

                fv = [0]

                def step(ins):
                    ins.then_inc(f_v, 1)
                    fv[0] += 1

                def last():
                    dve.wait_ge(f_v, at(b, N_FV, fv[0]))
                dve.wait_ge(f_mm, at(b, TB, TB))
                step(nc.vector.tensor_copy(lg[:, :, :], mx[:, :, 0:NE]))
                last()
                held(dve)
                for tb in range(TB):
                    step(nc.vector.max(top8[:, tb, :], lg[:, tb, :]))
                last()
                held(dve)
                for tb in range(TB):
                    step(nc.vector.max_index(idx8[:, tb, :], top8[:, tb, :], lg[:, tb, :]))
                last()
                step(nc.vector.tensor_copy(idxf[:, :, :], idx8[:, :, :]))
                step(nc.vector.tensor_tensor(dv21[:, :], top8[:, :, 1], top8[:, :, 0], ALU.subtract))
                assert fv[0] == 7
                dve.wait_ge(f_e, at(b, 1, 1))
                step(nc.vector.tensor_scalar(den1[:, :], e21[:, :], 1.0, None, ALU.add))
                last()
                step(nc.vector.reciprocal(p1[:, :], den1[:, :]))
                last()
                step(nc.vector.tensor_scalar(p1s[:, :], p1[:, :], LORA_SCALING, None, ALU.mult))
                last()
                step(nc.vector.tensor_tensor(p2s[:, :], e21[:, :], p1s[:, :], ALU.mult))
                last()
                iota = cst[:, C_IOTA:C_IOTA + NE]
                for tb in range(TB):
                    for gk, ps, k in ((g1, p1s, 0), (g2, p2s, 1)):
                        step(nc.vector.tensor_scalar(gk[:, tb, :], iota, idxf[:, tb, k:k + 1], ps[:, tb:tb + 1],
                                                     ALU.is_equal, ALU.mult))
                last()
                step(nc.vector.tensor_tensor(gate[:, :, :], g1[:, :, :], g2[:, :, :], ALU.add))
                last()
                for tb in range(TB):
                    step(nc.vector.tensor_tensor(hg[:, tb, :].rearrange("p (e r) -> p e r", r=RANK),
                                                 mx[:, tb, NE:GA].rearrange("p (e r) -> p e r", r=RANK),
                                                 gate[:, tb, :].unsqueeze(2).broadcast_to([P, NE, RANK]), ALU.mult))
                assert fv[0] == N_FV, fv
                dve.wait_ge(f_o, at(b, TB, TB))
                layernorm(b, 2, lambda tb: nc.vector.tensor_tensor(xres[:, tb, :], xres[:, tb, :], bank[tb][:, :], ALU.add))

        @block.tensor
        def _(pe):
            for s_, n in ((xt_ps, 4), (f_mm, TB), (f_base, 1), (f_t, TB), (f_o, TB), (s_qkv, 5), (s_sc, HB), (s_tp, HB), (s_pv, HB),
                          (s_y, 2), (wo_used, 4), (job, NJ), (mx_mm, HALVES * PAIRS), (mt_mm, HALVES), (sc_mm, NT),
                          (pv_mm, NT), (den_mm, HALVES)):
                pe.sem_inc(s_, n)
            pe.wait_ge(c_ld, N_CONST)
            pe.wait_ge(c_set, 8)

            def mm(dst, lhs, rhs, first, final):
                return nc.tensor.matmul(dst, lhs, rhs, start=first, stop=final)

            def transpose_x(b, k):
                pe.wait_ge(ln, at(b, 3 * N_LN, N_LN * (k + 1)))
                for tb in range(TB):
                    for c in range(DC):
                        tr = nc.tensor.transpose(bank[tb][:, c * P:(c + 1) * P], xres[:, tb, c * P:(c + 1) * P], ident)
                    tr.then_inc(xt_ps, 1)

            with pe.Fori(0, nb) as b:
                pe.wait_ge(xt_ld, at(b, 16, 16))
                held(pe)
                pe.wait_ge(ln, at(b, 3 * N_LN, 2 - N_LN))
                held(pe)
                with pe.Fori(0, NM) as m:
                    t = b * NM + m
                    pe.wait_ge(wq1_ld, at(t, 16, 16))
                    pe.wait_ge(s_res, at(t, 2, 0))
                    pe.wait_ge(s_exp, at(t, 2 * HB, 0))
                    for kind in range(2):
                        for c in range(DC):
                            last = mm(bank[kind][:, 0:S], wqkv[:, kind * D + c * P:kind * D + (c + 1) * P], xt[:, c, :],
                                      c == 0, c == DC - 1)
                        last.then_inc(s_qkv, 1)
                    for tb in range(TB):
                        for c in range(DC):
                            last = mm(bank[2][:, tb * P:(tb + 1) * P], xt[:, c, tb * P:(tb + 1) * P],
                                      wqkv[:, 2 * D + c * P:2 * D + (c + 1) * P], c == 0, c == DC - 1)
                    last.then_inc(s_qkv, 1)
                    for kind in range(2):
                        pe.wait_ge(s_qkb, at(t, 2, kind + 1))
                        mm(bank[kind][:, S:2 * S], swap[:, :], qkb[:, kind, :], True, True).then_inc(s_qkv, 1)
                    pe.wait_ge(s_rope, at(t, N_ROPE, 6))
                    pe.wait_ge(s_ot, at(t, 1, 0))
                    for h in range(HB + 3):
                        if h < HB:
                            sc = s_bank[h % 3]
                            pe.wait_ge(s_qm, at(t, HB, h + 1))
                            pe.wait_ge(s_exp, at(t, 2 * HB, 2 * h - 4))
                            if h == 2:
                                pe.wait_ge(s_rope, at(t, N_ROPE, N_ROPE))
                            for qb, a in ((0, 0), (1, 128)):
                                w = (qb + 1) * P
                                mm(sc[:, a:a + w], qm[:, h % 2, qb * P:(qb + 1) * P], kr[:, 0:w], True, False)
                                last = mm(sc[:, a + w - P:a + w], identb[:, :], maskb[:, :], False, True)
                            last.then_inc(s_sc, 1)
                        if 2 <= h < HB + 2:
                            k = h - 2
                            pe.wait_ge(s_pn, at(t, 2 * HB, 2 * k + 2))
                            pe.wait_ge(s_ptc, at(t, HB, k - 1))
                            for a in (0, 128, 256):
                                last = nc.tensor.transpose(pv[:, k % 2, a:a + P], pn[:, k % 3, a:a + P], ident)
                            last.then_inc(s_tp, 1)
                        if h >= 3:
                            k = h - 3
                            pe.wait_ge(s_ptc, at(t, HB, k + 1))
                            pe.wait_ge(s_rope, at(t, N_ROPE, N_ROPE))
                            mm(dn[:, 0:S], vx[:, 0, k * P:(k + 1) * P], pt[:, k % 2, 0:S], k == 0, False)
                            mm(dn[:, P:S], vx[:, 1, k * P:(k + 1) * P], pt[:, k % 2, S:S + P], False, k == HB - 1).then_inc(s_pv, 1)
                    pe.wait_ge(s_ot, at(t, 1, 1))
                    pe.wait_ge(wo1_ld, at(t, 16, 16))
                    for tb in range(TB):
                        mm(bank[tb][:, :], ots[:, tb * P:(tb + 1) * P], wos[:, 0:D], True, True).then_inc(s_y, 1)
                pe.wait_ge(s_res, at(b * NM + (NM - 1), 2, 2))
                transpose_x(b, 0)
                pe.wait_ge(split, at(b, N_STAGE, 5))
                pe.wait_ge(xt_ok, at(b, 4, 2))
                held(pe)
                with pe.Fori(0, NP) as p:
                    t = b * NP + p
                    pe.wait_ge(split, at(b, N_STAGE, 5) + p)

                    def max_pair(h, r):
                        kv, q0 = h // 2, (h % 2) * QH + (r // 2) * P
                        pe.wait_ge(mx_free, at(t, MXU, h * (PAIRS + 1) + r))
                        for half in range(2):
                            a, n = MCH[r % 2][half]
                            last = mm(mx[:, half, 0:n], qh[:, kv, q0:q0 + P], kh[:, kv, a:a + n], True, True)
                        last.then_inc(mx_mm, 1)

                    def transpose_max(h):
                        pe.wait_ge(m4_ok, at(t, HALVES, h + 1))
                        mm(mx[0:4, 0, 0:P], m4[:, h % 2, :], ident, True, True).then_inc(mt_mm, 1)

                    for j, (kind, kv, i) in enumerate(JOBS):
                        if j in MAX_AT:
                            if j == MAX_AT[0]:
                                pe.wait_ge(job_lo, at(t, NJ, 8))
                            max_pair(0, MAX_AT.index(j))
                        dst = bank[j % RING]
                        if j < RING:
                            pe.wait_ge(exp_ok, at(t, NT, j - RING + 1))
                        else:
                            pe.wait_ge(job_lo, at(t, NJ, j - RING + 1))
                        if kind == "K":
                            a, n = KCH[i]
                            w = slice(kv * P, (kv + 1) * P)
                            for c in range(DC):
                                mm(dst[:, 0:n], wkvh[:, c, w], ctxh[:, c, a:a + n], c == 0, False)
                                mm(dst[:, 0:n], wkvh[:, c, w], ctxl[:, c, a:a + n], False, False)
                                last = mm(dst[:, 0:n], wkvl[:, c, w], ctxh[:, c, a:a + n], False, c == DC - 1)
                        elif kind == "Q":
                            if i == 0:
                                pe.wait_ge(wq_ld, at(t, 32, 16 * (kv + 1)))
                            for c in range(DC):
                                last = mm(dst[:, 0:S], wqb[:, c, i * P:(i + 1) * P], xt[:, c, :], c == 0, c == DC - 1)
                        else:
                            n = LAST if i == KT - 1 else P
                            for c in range(DC):
                                keys = slice(i * P, i * P + n)
                                mm(dst[0:n, 0:256], ctxh[:, c, keys], wkvh[:, c, 256:512], c == 0, False)
                                mm(dst[0:n, 0:256], ctxh[:, c, keys], wkvl[:, c, 256:512], False, False)
                                last = mm(dst[0:n, 0:256], ctxl[:, c, keys], wkvh[:, c, 256:512], False, c == DC - 1)
                        last.then_inc(job, 1)
                        if j == MAX_AT[-1] + 2:
                            transpose_max(0)

                    def weigh(g):
                        h, i = divmod(g, KT)
                        kv, n = h // 2, LAST if i == KT - 1 else P
                        w = slice(kv * P, (kv + 1) * P)
                        if i == 0:
                            pe.wait_ge(on_ok, at(t, HALVES, h - 1))
                        pe.wait_ge(lo_ok, at(t, NT, g + 1))
                        dst = pv[:, h % 2, :]
                        mm(dst, vh[0:n, i, w], ph[0:n, g % 2, :], i == 0, False)
                        mm(dst, vh[0:n, i, w], pl[0:n, g % 2, :], False, False)
                        mm(dst, vl[0:n, i, w], ph[0:n, g % 2, :], False, i == KT - 1).then_inc(pv_mm, 1)

                    def denominators(h):
                        pe.wait_ge(sum_ok, at(t, HALVES * (KT - 1), (h + 1) * (KT - 1)))
                        pe.wait_ge(rden_ok, at(t, 4 * HALVES, 4 * h))
                        mm(dn[:, :], ones[:, :], psm[:, h % 2, :], True, True).then_inc(den_mm, 1)

                    def project(c, k):
                        if c == 0 and k == 0:
                            pe.wait_ge(mx_free, at(t, MXU, MXU - 1))
                        if k == 0:
                            pe.wait_ge(wo_ld[c % 2], at(t, 32, 16 * (c // 2 + 1)))
                            pe.wait_ge(ot_ok, at(t, HALVES, c + 1))
                        for tb in range(TB):
                            last = mm(mx[:, tb, :], ot[:, 2 * c + k, tb * P:(tb + 1) * P], wob[:, c % 2, k, :],
                                      c == 0 and k == 0, c == 3 and k == 1)
                        if k == 1:
                            last.then_inc(wo_used, 1)

                    for g in range(NT):
                        h, i = divmod(g, KT)
                        kv, q0 = h // 2, (h % 2) * QH
                        n = LAST if i == KT - 1 else P
                        keys, cols = slice(i * P, i * P + n), slice(q0, q0 + QH)
                        u = NJ + g
                        if h + 1 < HALVES and i < PAIRS:
                            max_pair(h + 1, i)
                        dst = bank[u % RING][0:n, :]
                        if g < RING:
                            pe.wait_ge(job_lo, at(t, NJ, NJ + g - RING + 1))
                        else:
                            pe.wait_ge(exp_ok, at(t, NT, g - RING + 1))
                        if i == 0:
                            pe.wait_ge(shift_ok, at(t, HALVES, h + 1))
                        mm(dst, kh[:, kv, keys], qh[:, kv, cols], True, False)
                        mm(dst, kh[:, kv, keys], ql[:, kv, cols], False, False)
                        mm(dst, kl[:, kv, keys], qh[:, kv, cols], False, False)
                        mm(dst, negones[:, 0:n], shift[:, h % 2, :, :].rearrange("p a c -> p (a c)"), False, True).then_inc(sc_mm, 1)
                        if g >= 2:
                            weigh(g - 2)
                        if h + 1 < HALVES and i == PAIRS + 1:
                            transpose_max(h + 1)
                        if h == HALVES - 1 and i in (6, 8):
                            project(0, (i - 6) // 2)
                        if h >= 1 and i == 3:
                            denominators(h - 1)
                    project(1, 0)
                    weigh(NT - 2)
                    project(1, 1)
                    weigh(NT - 1)
                    denominators(HALVES - 1)
                    for c in (2, 3):
                        project(c, 0)
                        project(c, 1)
                transpose_x(b, 1)
                pe.wait_ge(f_ld, at(b, 64, 64))
                pe.wait_ge(xt_ok, at(b, 4, 4))
                for tb in range(TB):
                    rows = slice(tb * P, (tb + 1) * P)
                    for c in range(DC):
                        last = mm(mx[:, tb, 0:GA], xt[:, c, rows], wgat[:, c, :], c == 0, c == DC - 1)
                    last.then_inc(f_mm, 1)
                for tb in range(TB):
                    for c in range(DC):
                        last = mm(bank[tb][:, :], xt[:, c, tb * P:(tb + 1) * P], wbt[:, c, :], c == 0, False)
                last.then_inc(f_base, 1)
                pe.wait_ge(f_v, at(b, N_FV, N_FV))
                for tb in range(TB):
                    for k, n in enumerate((P, ER - P)):
                        last = nc.tensor.transpose(pv[0:n, tb, k * P:(k + 1) * P], hg[:, tb, k * P:k * P + n], ident)
                    last.then_inc(f_t, 1)
                for tb in range(TB):
                    pe.wait_ge(f_tc, at(b, 4, 2 * tb + 2))
                    mm(bank[tb][:, :], hgt[:, tb, 0, :], wlbt[:, 0, :], False, False)
                    mm(bank[tb][:, :], hgt[0:ER - P, tb, 1, :], wlbt[0:ER - P, 1, :], False, True).then_inc(f_o, 1)


_OUT = ((B, TB, P, D), "float32")


def kernel(**inputs):
    import concourse.bacc as bacc
    from concourse.bass_utils import run_bass_kernel_spmd

    nc = bacc.Bacc("TRN2", target_bir_lowering=False, num_devices=1)
    arrays = lay_out({k: np.asarray(v) for k, v in inputs.items()})
    args = {n: nc.dram_tensor(f"in_{n}", a.shape, mybir.dt.from_np(a.dtype), kind="ExternalInput").ap()
            for n, a in arrays.items()}
    o = nc.dram_tensor("out", (B, P, TB, D), F32, kind="ExternalOutput").ap()
    build(nc, **args, out=o)
    r = run_bass_kernel_spmd(nc, [{f"in_{n}": a for n, a in arrays.items()}], core_ids=[0])
    return np.ascontiguousarray(r.results[0]["out"].transpose(0, 2, 1, 3)).reshape(B, S, D)


def lay_out(i):
    c = np.ascontiguousarray
    kinds = [(i["L0_attn_Wq"], i["L0_attn_bq"]), (i["L0_attn_Wk"], i["L0_attn_bk"]), (i["L0_attn_Wv"], i["L0_attn_bv"])]
    ws = np.zeros((NM, P, W_QKV + D + 1), np.float32)
    for m in range(NM):
        rows = slice(m * P, (m + 1) * P)
        for k, (w, bias) in enumerate(kinds):
            ws[m, :, k * D:(k + 1) * D] = w[rows].T.reshape(DC, P, P).transpose(1, 0, 2).reshape(P, D)
            ws[m, :, 3 * D + k if k < 2 else W_QKV + D] = bias[rows]
        ws[m, :, W_QKV:W_QKV + D] = i["L0_attn_Wo"].T[rows]
    w = i["L0_xattn_Wkv"].reshape(DC, P, 2, NP, 2 * XD).transpose(3, 1, 0, 2, 4).reshape(NP, P, DC * 4 * XD)
    wkv = c(np.concatenate([w, w[:1]]))
    wq = c(i["L0_xattn_Wq"].reshape(DC, P, XKV, G * XD).transpose(2, 1, 0, 3))
    wo = c(i["L0_xattn_Wo"].reshape(XH // 2, 2, P, D).transpose(0, 2, 1, 3))
    rows_b = lambda v: c(np.broadcast_to(v, (P, D)))
    wga = np.concatenate([i["L0_ffn_gate_W"], i["L0_ffn_lora_A"].reshape(ER, D)])
    wlb = np.zeros((2, P, D), np.float32)
    lb = i["L0_ffn_lora_B"].transpose(0, 2, 1).reshape(ER, D)
    wlb[0], wlb[1, :ER - P] = lb[:P], lb[P:]
    theta = (1.0 / 10000.0 ** (np.arange(0, DH, 2, dtype=np.float32) / DH)).astype(np.float32)
    ang = (np.arange(S, dtype=np.float32)[:, None] * theta[None, :]).astype(np.float32)
    d = np.arange(P) % DH
    sign = np.where(d % 2 == 0, -1.0, 1.0).astype(np.float32)
    rope = np.stack([np.cos(ang).T[d // 2], np.sin(ang).T[d // 2] * sign[:, None]], axis=1).astype(np.float32)
    consts = np.zeros((P, C_N), np.float32)
    consts[:, C_ID:C_ID + P] = np.eye(P)
    consts[:, C_SW:C_SW + P] = np.eye(P)[np.arange(P) ^ 1]
    consts[:, C_HM:C_HM + HB] = np.arange(P)[:, None] // DH == np.arange(HB)
    consts[:, C_IOTA:C_IOTA + NE] = np.arange(NE)
    consts[:, C_EPS] = EPS
    consts[:, C_BK:C_BK + XKV] = i["L0_xattn_bkv"][:XKV * XD].reshape(XKV, XD).T
    consts[:, C_BV:C_BV + XKV] = i["L0_xattn_bkv"][XKV * XD:].reshape(XKV, XD).T
    consts[:, C_BQ:C_BQ + XH] = i["L0_xattn_bq"].reshape(XH, XD).T
    bmask = c(np.broadcast_to(np.eye(4, dtype=np.float32)[:, :, None], (4, 4, P)))
    again = lambda v: c(np.concatenate([v, v[:1]]))
    return dict(
        x=again(i["x"].reshape(B, TB, P, D).transpose(0, 2, 1, 3)),
        x_t=again(i["x"].reshape(B, S, DC, P).transpose(0, 3, 2, 1)),
        ctx_t=c(i["ctx_4096"].reshape(B, LK, DC, P).transpose(0, 2, 3, 1)),
        ws=ws, wkv=wkv, wq=wq, wo=wo, bo_s=rows_b(i["L0_attn_bo"]), bo_x=rows_b(i["L0_xattn_bo"]),
        wb=c(i["L0_ffn_base_W"].T.reshape(DC, P, D).transpose(1, 0, 2)),
        wga=c(wga.T.reshape(DC, P, GA).transpose(1, 0, 2)), wlb=c(wlb.transpose(1, 0, 2)),
        rope=rope, consts=consts, bmask=bmask)
```

```python
from contextlib import ExitStack

import numpy as np

import concourse.bass as bass
from concourse import mybir

F32 = mybir.dt.float32
F32R = mybir.dt.float32r
BF16 = mybir.dt.bfloat16
U32 = mybir.dt.uint32
ALU = mybir.AluOpType
ACT = mybir.ActivationFunctionType
AX = mybir.AxisListType

P = 128
B, S, D = 4, 256, 512
DC = D // P
TB = S // P
NH, DH = 32, 16
HB = P // DH
NM = NH // HB
XH, XKV, XD = 32, 8, 128
G = XH // XKV
NP = XKV // 2
LK = 1601
KT = (LK + P - 1) // P
LAST = LK - (KT - 1) * P
LKP = LK + 1
NE, RANK = 28, 8
ER = NE * RANK
LORA_SCALING = 16 / 8
GA = NE + ER
EPS = 1e-5
NEG = -1.0e30
XSCALE = 1.0 / float(np.sqrt(XD))
SSCALE = 1.0 / float(np.sqrt(DH))

KCH = [(0, 400), (400, 400), (800, 400), (1200, 402)]
MCH = [((0, 400), (400, 400), 400), ((800, 402), (1200, 402), 401)]

PIECES = 4
CTX_PIECES = [(0, 400), (400, 800), (800, 1200), (1200, LK)]
WKV_AT = (3, 5, 7, 9)

JOBS = [("K", 0, j) for j in range(4)] + [("Q", 0, g) for g in range(G)] \
    + [("K", 1, j) for j in range(4)] + [("Q", 1, g) for g in range(G)] + [("V", 0, t) for t in range(KT)]
NJ = len(JOBS)
HALVES = 4
NT = HALVES * KT
QH = 2 * S
RING = 3
assert (NJ + NT) % RING == 0 and NT % 2 == 0
PAIRS = 8
MXU = HALVES * (PAIRS + 1) + 1
MAX_AT = (10, 12, 14, 16, 18, 20, 22, 24)
EARLY_AT = NJ - 1


def pair_at(g):
    h, i = divmod(g, KT)
    if h == 0 and i < 2:
        return (1, 1) if i == 0 else None
    return (h + 1, i) if h + 1 < HALVES and i < PAIRS else None


def ends_at(h):
    return PAIRS - 1 if h < HALVES - 1 else 4


C_ID, C_HM, C_IOTA, C_EPS, C_BK, C_BV, C_BQ, C_SW = 0, 128, 136, 164, 165, 173, 181, 213
C_N = C_SW + P
W_QKV = 3 * D + 2


def at(turn, per_turn, n):
    return turn * per_turn + (per_turn + n)


def build(nc, x, x_t, ctx_t, ws, wkv, wq, wo, bo_s, bo_x, wb, wga, wlb, rope, consts, bmask, out, nb=B):
    with ExitStack() as ctx:
        def sb(name, shape, dt=F32, stack=ctx):
            return stack.enter_context(nc.sbuf_tensor(name, shape, dt))

        def sem(name):
            return ctx.enter_context(nc.semaphore(name))

        cst = sb("cst", [P, C_N])
        ones = sb("ones", [P, P])
        identb = sb("identb", [P, P], BF16)
        maskb = sb("maskb", [P, P], BF16)
        negones = sb("negones", [4, P], F32R)
        blockm = sb("blockm", [4, 4, P])
        xres = sb("xres", [P, TB, D])
        xt = sb("xt", [P, DC, S])
        stats = sb("stats", [P, TB, 6])
        mv = sb("mv", [P, TB, 2])
        rstd = sb("rstd", [P, TB])
        ctxh = sb("ctxh", [P, DC, LKP], F32R)
        ctxl = sb("ctxl", [P, DC, LKP], F32R)
        stage = sb("stage", [P, DC * 512])
        wkvh = sb("wkvh", [P, DC, 512], F32R)
        wkvl = sb("wkvl", [P, DC, 512], F32R)
        box = sb("box", [P, D])
        ident = cst[:, C_ID:C_ID + P]
        swap = cst[:, C_SW:C_SW + P]

        with ExitStack() as st:
            wbt = sb("wbt", [P, DC, D], stack=st)
            wgat = sb("wgat", [P, DC, GA], stack=st)
            wlbt = sb("wlbt", [P, 2, D], stack=st)
            lg = sb("lg", [P, TB, NE], stack=st)
            top8 = sb("top8", [P, TB, 8], stack=st)
            idx8 = sb("idx8", [P, TB, 8], U32, stack=st)
            idxf = sb("idxf", [P, TB, 8], stack=st)
            dv21 = sb("dv21", [P, TB], stack=st)
            e21 = sb("e21", [P, TB], stack=st)
            den1 = sb("den1", [P, TB], stack=st)
            p1 = sb("p1", [P, TB], stack=st)
            p1s = sb("p1s", [P, TB], stack=st)
            p2s = sb("p2s", [P, TB], stack=st)
            g1 = sb("g1", [P, TB, NE], stack=st)
            g2 = sb("g2", [P, TB, NE], stack=st)
            gate = sb("gate", [P, TB, NE], stack=st)
            hg = sb("hg", [P, TB, ER], stack=st)
            hgt = sb("hgt", [P, TB, 2, P], stack=st)
            wqkv = sb("wqkv", [P, W_QKV], stack=st)
            wos = sb("wos", [P, D + 1], stack=st)
            qkb = sb("qkb", [P, 2, S], stack=st)
            rp = sb("rp", [P, 2, S], stack=st)
            bos = sb("bos", [P, D], stack=st)
            qr = sb("qr", [P, S], stack=st)
            kr = sb("kr", [P, S], stack=st)
            t1 = sb("t1", [P, S], stack=st)
            t2 = sb("t2", [P, S], stack=st)
            qm = sb("qm", [P, 2, S], stack=st)
            vx = sb("vx", [P, TB, HB * (P + DH)], stack=st)
            pn = sb("pn", [P, 3, 384], stack=st)
            pt = sb("pt", [P, 2, 384], stack=st)
            nmx = sb("nmx", [P, 3, 2], stack=st)
            sm = sb("sm", [P, 3, 2], stack=st)
            rsm = sb("rsm", [P, 3, 2], stack=st)
            ots = sb("ots", [P, S], stack=st)
        kh = sb("kh", [P, 2, LKP], F32R)
        kl = sb("kl", [P, 2, LKP], F32R)
        vh = sb("vh", [P, KT, 256], F32R)
        vl = sb("vl", [P, KT, 256], F32R)
        qh = sb("qh", [P, 2, G * S], F32R)
        ql = sb("ql", [P, 2, G * S], F32R)
        wqb = sb("wqb", [P, DC, G * XD])
        wob = sb("wob", [P, 4, D])
        p32 = sb("p32", [P, 2, QH])
        ph = sb("ph", [P, 2, QH], F32R)
        pl = sb("pl", [P, 2, QH], F32R)
        psm = sb("psm", [P, 2, QH])
        rden = sb("rden", [P, QH])
        ot = sb("ot", [P, 2 * G, S])
        shift = sb("shift", [4, 2, 4, P], F32R)
        mxp = sb("mxp", [P, 2, PAIRS])
        m4 = sb("m4", [P, 2, 4])

        bank = [ctx.enter_context(nc.psum_tensor(f"bank{i}", [P, 512], F32)) for i in range(RING)]
        mx = ctx.enter_context(nc.psum_tensor("mx", [P, 2, 512], F32))
        pv = ctx.enter_context(nc.psum_tensor("pv", [P, 2, 512], F32))
        dn = ctx.enter_context(nc.psum_tensor("dn", [P, 512], F32))
        s_bank = [mx[:, 0, :], mx[:, 1, :], bank[2][:, :]]

        c_ld, c_set, phase, passed = (sem(n) for n in ("c_ld", "c_set", "phase", "passed"))
        x_ld, xt_ld, rp_ld, f_ld, stage_ld, split, stored = (sem(n) for n in ("x_ld", "xt_ld", "rp_ld", "f_ld", "stage_ld", "split", "stored"))
        split_hi, split_lo, xr_ok, bias_ok, f_res = (sem(n) for n in ("split_hi", "split_lo", "xr_ok", "bias_ok", "f_res"))
        ln, ln_sd, xt_ps, xt_ok = (sem(n) for n in ("ln", "ln_sd", "xt_ps", "xt_ok"))
        f_mm, f_base, f_v, f_e, f_t, f_tc, f_o = (sem(n) for n in ("f_mm", "f_base", "f_v", "f_e", "f_t", "f_tc", "f_o"))
        wq1_ld, wo1_ld, s_qkv, s_qkb, s_rope, s_v, s_vz = (sem(n) for n in ("wq1_ld", "wo1_ld", "s_qkv", "s_qkb", "s_rope", "s_v", "s_vz"))
        s_qm, s_sc, s_mx, s_exp, s_rs, s_pn = (sem(n) for n in ("s_qm", "s_sc", "s_mx", "s_exp", "s_rs", "s_pn"))
        s_tp, s_ptc, s_pv, s_ot, s_y, s_res = (sem(n) for n in ("s_tp", "s_ptc", "s_pv", "s_ot", "s_y", "s_res"))
        wq_ld, wo_ld, wo_used = sem("wq_ld"), [sem(f"wo_ld{n}") for n in range(4)], sem("wo_used")
        job, job_hi, job_lo = sem("job"), sem("job_hi"), sem("job_lo")
        mx_mm, mx_free, m4_ok, mt_mm, shift_ok = (sem(n) for n in ("mx_mm", "mx_free", "m4_ok", "mt_mm", "shift_ok"))
        sc_mm, exp_ok, hi_ok, lo_ok, sum_ok, pv_mm = (sem(n) for n in ("sc_mm", "exp_ok", "hi_ok", "lo_ok", "sum_ok", "pv_mm"))
        den_mm, rden_ok, on_ok, ot_ok = (sem(n) for n in ("den_mm", "rden_ok", "on_ok", "ot_ok"))

        N_STAGE = 4 + NP
        N_CONST = 3 * 16
        N_ROPE = 6
        N_LN = 7
        N_FV = 7 + 4 + 2 * TB + 1 + TB

        def held(eng):
            eng.sem_inc(passed, 1)

        block = ctx.enter_context(nc.Block())

        @block.sync
        def _(sp):
            sp.dma_start(cst[:, :], consts).then_inc(c_ld, 16)
            sp.dma_start(blockm[:, :, :], bmask).then_inc(c_ld, 16)
            sp.dma_start(box[:, :], bo_x).then_inc(c_ld, 16)
            for s_, n in ((x_ld, 32), (xt_ld, 16), (rp_ld, 16), (f_ld, 48), (stage_ld, 16 * N_STAGE),
                          (wq1_ld, 16), (wo1_ld, 16), (wq_ld, 32), *((s_, 32) for s_ in wo_ld), (stored, 16)):
                sp.sem_inc(s_, n)

            def first_weights():
                sp.dma_start(wqkv[:, :], ws[0, :, 0:W_QKV]).then_inc(wq1_ld, 16)
                sp.dma_start(rp[:, :, :], rope).then_inc(rp_ld, 16)
                sp.dma_start(wos[:, :], ws[0, :, W_QKV:W_QKV + D + 1]).then_inc(wo1_ld, 16)
                sp.dma_start(bos[:, :], bo_s).then_inc(x_ld, 16)

            sp.dma_start(xt[:, :, :], x_t[0]).then_inc(xt_ld, 16)
            first_weights()
            sp.dma_start(xres[:, :, :], x[0]).then_inc(x_ld, 16)
            sp.dma_start(stage[:, :], wkv[0]).then_inc(stage_ld, 16)
            with sp.Fori(0, nb) as b:
                with sp.Fori(0, NM - 1) as m:
                    t = b * NM + m
                    sp.wait_ge(split, at(b, N_STAGE, 1) + m)
                    held(sp)
                    sp.dma_start(stage[:, 0:LK], ctx_t[b, m]).then_inc(stage_ld, 16)
                    sp.wait_ge(s_qkv, at(t, 5, 5))
                    held(sp)
                    sp.wait_ge(s_qkb, at(t, 2, 2))
                    held(sp)
                    sp.dma_start(wqkv[:, :], ws[m + 1, :, 0:W_QKV]).then_inc(wq1_ld, 16)
                    sp.wait_ge(s_y, at(t, 2, 2))
                    held(sp)
                    sp.dma_start(wos[:, :], ws[m + 1, :, W_QKV:W_QKV + D + 1]).then_inc(wo1_ld, 16)
                sp.wait_ge(split, at(b, N_STAGE, NM))
                sp.dma_start(stage[:, 0:LK], ctx_t[b, NM - 1]).then_inc(stage_ld, 16)
                sp.wait_ge(xt_ps, at(b, 4, 2))
                held(sp)
                with sp.Fori(0, NP) as p:
                    t = b * NP + p
                    for kv in range(2):
                        sp.wait_ge(job, at(t, NJ, 0) if kv == 0 else at(t, NJ, 8))
                        sp.dma_start(wqb[:, :, :], wq[2 * p + kv]).then_inc(wq_ld, 16)
                    sp.wait_ge(split, at(b, N_STAGE, 5) + p)
                    sp.dma_start(stage[:, :], wkv[p + 1]).then_inc(stage_ld, 16)
                    for n in range(2 * G):
                        sp.wait_ge(wo_used, at(t, 2 * G, n - 3))
                        sp.dma_start(wob[:, n % 4, :], wo[2 * G * p + n]).then_inc(wo_ld[n % 4], 16)
                sp.wait_ge(sc_mm, at(b * NP + (NP - 1), NT, NT))
                held(sp)
                sp.dma_start(wgat[:, :, :], wga).then_inc(f_ld, 16)
                sp.dma_start(wbt[:, :, :], wb).then_inc(f_ld, 16)
                sp.dma_start(wlbt[:, :, :], wlb).then_inc(f_ld, 16)
                sp.wait_ge(wo_used, at(b * NP + (NP - 1), 2 * G, 2 * G))
                held(sp)
                first_weights()
                sp.wait_ge(f_base, at(b, 1, 1))
                held(sp)
                sp.dma_start(xt[:, :, :], x_t[b + 1]).then_inc(xt_ld, 16)
                sp.wait_ge(ln, at(b, 3 * N_LN, 3 * N_LN))
                held(sp)
                sp.dma_start(out[b], xres[:, :, :]).then_inc(stored, 16)
                sp.wait_ge(stored, at(b, 16, 16))
                held(sp)
                sp.dma_start(xres[:, :, :], x[b + 1]).then_inc(x_ld, 16)
            for load, primed, in_sequence in ((x_ld, 32, 32), (xt_ld, 16, 16), (rp_ld, 16, 16), (wq1_ld, 16, 16 * NM),
                                              (wo1_ld, 16, 16 * NM), (stage_ld, 16 * N_STAGE, 16 * N_STAGE)):
                sp.wait_ge(load, primed + nb * in_sequence + (32 if load is x_ld else 16))

        @block.gpsimd
        def _(pool):
            nc.gpsimd.memset(ones[:, :], 1.0).then_inc(c_set, 1)
            nc.gpsimd.memset(negones[:, :].bitcast(F32), -1.0).then_inc(c_set, 1)
            nc.gpsimd.memset(ctxh[:, :, LK:LKP].bitcast(F32), 0.0).then_inc(c_set, 1)
            nc.gpsimd.memset(ctxl[:, :, LK:LKP].bitcast(F32), 0.0).then_inc(c_set, 1)
            nc.gpsimd.memset(identb[:, :], 0.0).then_inc(c_set, 1)
            nc.gpsimd.memset(maskb[:, :], 0.0).then_inc(c_set, 1)
            pool.wait_ge(c_set, 6)
            nc.gpsimd.affine_select(out=identb[:, :], in_=identb[:, :], compare_op=ALU.not_equal, fill=1.0,
                                    base=0, pattern=[[-1, P]], channel_multiplier=1).then_inc(c_set, 1)
            nc.gpsimd.affine_select(out=maskb[:, :], in_=maskb[:, :], compare_op=ALU.is_ge, fill=NEG,
                                    base=0, pattern=[[-1, P]], channel_multiplier=1).then_inc(c_set, 1)
            pool.sem_inc(split, N_STAGE)
            pool.sem_inc(bias_ok, 2 * TB)
            pool.wait_ge(c_ld, N_CONST)
            pool.sem_inc(sum_ok, HALVES * (KT - 1))
            nc.gpsimd.memset(vx[:, :, :], 0.0).then_inc(s_vz, 1)
            wstage = stage[:, :].rearrange("p (c n) -> p c n", c=DC)

            def low_part(k, lo, hi, src, n):
                pool.wait_ge(split_hi, n * PIECES + k + 1)
                part = nc.gpsimd.tensor_tensor(lo, src, hi, ALU.subtract)
                part.then_inc(split_lo, 1)
                if k == PIECES - 1:
                    pool.wait_ge(split_lo, (n + 1) * PIECES)
                    pool.sem_inc(split, 1)

            for k in range(PIECES):
                low_part(k, wkvl[:, k, :], wkvh[:, k, :], wstage[:, k, :], 0)
            with pool.Fori(0, nb) as b:
                pool.wait_ge(x_ld, at(b, 32, 32))
                for tb in range(TB):
                    nc.gpsimd.tensor_tensor(xres[:, tb, :], xres[:, tb, :], bos[:, :], ALU.add).then_inc(bias_ok, 1)
                with pool.Fori(0, DC) as c:
                    for k, (a, z) in enumerate(CTX_PIECES):
                        low_part(k, ctxl[:, c, a:z], ctxh[:, c, a:z], stage[:, a:z], b * N_STAGE + c + 1)
                pool.wait_ge(xt_ps, at(b, 2 * TB, TB))
                for tb in range(TB):
                    nc.gpsimd.tensor_tensor(xres[:, tb, :], xres[:, tb, :], box[:, :], ALU.add).then_inc(bias_ok, 1)
                with pool.Fori(0, NP) as p:
                    t = b * NP + p
                    for h in range(HALVES):
                        acc = psm[:, h % 2, :]
                        pool.wait_ge(den_mm, at(t, HALVES, h - 1))
                        for i in range(1, KT):
                            n = LAST if i == KT - 1 else P
                            g = h * KT + i
                            pool.wait_ge(exp_ok, at(t, NT, g + 1))
                            if i == 1:
                                add = nc.gpsimd.tensor_tensor(acc, p32[:, (g - 1) % 2, :], p32[:, g % 2, :], ALU.add)
                            else:
                                pool.wait_ge(sum_ok, at(t, HALVES * (KT - 1), h * (KT - 1) + i - 1))
                                add = nc.gpsimd.tensor_tensor(acc[0:n], acc[0:n], p32[0:n, g % 2, :], ALU.add)
                            add.then_inc(sum_ok, 1)
                            if h == 1 and i in WKV_AT:
                                k = WKV_AT.index(i)
                                low_part(k, wkvl[:, k, :], wkvh[:, k, :], wstage[:, k, :], b * N_STAGE + 5 + p)
                pool.wait_ge(wo_used, at(b * NP + (NP - 1), 2 * G, 2 * G))
                held(pool)
                nc.gpsimd.memset(vx[:, :, :], 0.0).then_inc(s_vz, 1)

        def sums_after(g):
            h, i = divmod(g, KT)
            return h * (KT - 1) + max(i, 1)

        def add_bv(act, t, p, h):
            for k in range(2):
                act.wait_ge(on_ok, at(t, 2 * HALVES, 2 * h + k + 1))
                held(act)
                nc.scalar.activation(ot[:, 2 * h + k, :], ot[:, 2 * h + k, :], ACT.Identity,
                                     bias=cst[:, bass.ds(2 * p + (C_BV + h // 2), 1)]).then_inc(ot_ok, 1)

        @block.scalar
        def _(act):
            for s_, n in ((ln_sd, 3), (xt_ok, 4), (f_e, 1), (f_tc, 4), (s_exp, 2 * HB), (s_ptc, HB), (s_ot, 1), (s_qkb, 2), (s_v, 2),
                          (job_hi, NJ), (exp_ok, NT), (hi_ok, NT), (ot_ok, 2 * HALVES)):
                act.sem_inc(s_, n)
            act.wait_ge(c_ld, N_CONST)

            def deviation(b, k):
                act.wait_ge(ln, at(b, 3 * N_LN, N_LN * k + 4))
                nc.scalar.activation(rstd[:, :], mv[:, :, 1], ACT.Sqrt, bias=cst[:, C_EPS:C_EPS + 1]).then_inc(ln_sd, 1)

            def copy_xt(b, k):
                for tb in range(TB):
                    act.wait_ge(xt_ps, at(b, 2 * TB, TB * k + tb + 1))
                    nc.scalar.activation(xt[:, :, tb * P:(tb + 1) * P],
                                         mx[:, tb, :].rearrange("p (c n) -> p c n", c=DC), ACT.Copy).then_inc(xt_ok, 1)

            def high_part(hi, src):
                nc.scalar.activation(hi, src, ACT.Copy).then_inc(split_hi, 1)

            wstage = stage[:, :].rearrange("p (c n) -> p c n", c=DC)
            act.wait_ge(stage_ld, 16 * N_STAGE + 16)
            for k in range(PIECES):
                high_part(wkvh[:, k, :], wstage[:, k, :])

            with act.Fori(0, nb) as b:
                act.wait_ge(s_vz, b + 1)
                held(act)
                with act.Fori(0, NM) as m:
                    t = b * NM + m
                    act.wait_ge(wq1_ld, at(t, 16, 16))
                    for k in range(2):
                        act.wait_ge(s_qkv, at(t, 5, k + 1))
                        act.wait_ge(s_rope, at(t, N_ROPE, 3 * k - 2))
                        nc.scalar.activation(qkb[:, k, :], bank[k][:, 0:S],
                                             ACT.Identity, bias=wqkv[:, 3 * D + k:3 * D + k + 1]).then_inc(s_qkb, 1)
                    act.wait_ge(s_qkv, at(t, 5, 5))
                    act.wait_ge(s_pv, at(t, HB, 0))
                    for tb in range(TB):
                        nc.scalar.activation(vx[:, tb, :].rearrange("p (h x) -> p h x", h=HB)[:, :, 0:DH],
                                             dn[:, S + tb * P:S + (tb + 1) * P].rearrange("p (h x) -> p h x", h=HB),
                                             ACT.Copy).then_inc(s_v, 1)
                    act.wait_ge(s_y, at(t, 2, 0))
                    for h in range(HB + 2):
                        if h < HB:
                            act.wait_ge(s_mx, at(t, 2 * HB, 2 * h + 2))
                            act.wait_ge(s_tp, at(t, HB, h - 2))
                            act.wait_ge(s_rs, at(t, HB, h - 2))
                            for qb, (a, z) in enumerate(((0, 128), (128, 384))):
                                nc.scalar.activation(pn[:, h % 3, a:z], s_bank[h % 3][:, a:z], ACT.Exp,
                                                     bias=nmx[:, h % 3, qb:qb + 1],
                                                     accum_out=sm[:, h % 3, qb:qb + 1]).then_inc(s_exp, 1)
                        if h >= 2:
                            k = h - 2
                            act.wait_ge(s_tp, at(t, HB, k + 1))
                            act.wait_ge(s_pv, at(t, HB, k - 1))
                            nc.scalar.activation(pt[:, k % 2, :], pv[:, k % 2, 0:384], ACT.Copy).then_inc(s_ptc, 1)
                        if h in (1, 3, 5, 7):
                            if h == 1:
                                act.wait_ge(stage_ld, 16 * (b * N_STAGE + m) + 16 * (N_STAGE + 2))
                                held(act)
                            a, z = CTX_PIECES[h // 2]
                            high_part(ctxh[:, bass.ds(m, 1), a:z], stage[:, a:z].unsqueeze(1))
                    act.wait_ge(s_pv, at(t, HB, HB))
                    act.wait_ge(wo1_ld, at(t, 16, 16))
                    nc.scalar.activation(ots[:, :], dn[:, 0:S], ACT.Identity, bias=wos[:, D:D + 1]).then_inc(s_ot, 1)
                deviation(b, 0)
                copy_xt(b, 0)
                with act.Fori(0, NP) as p:
                    t = b * NP + p
                    for j, (kind, kv, i) in enumerate(JOBS):
                        act.wait_ge(job, at(t, NJ, j + 1))
                        src = bank[j % RING]
                        if kind == "K":
                            a, n = KCH[i]
                            if i == 0 and kv == 0:
                                act.wait_ge(sc_mm, at(t, NT, 0))
                            held(act)
                            nc.scalar.activation(kh[:, kv, a:a + n], src[:, 0:n], ACT.Identity,
                                                 bias=cst[:, bass.ds(2 * p + (C_BK + kv), 1)]).then_inc(job_hi, 1)
                        elif kind == "Q":
                            held(act)
                            nc.scalar.activation(qh[:, kv, i * S:(i + 1) * S], src[:, 0:S], ACT.Identity,
                                                 bias=cst[:, bass.ds(8 * p + (C_BQ + G * kv + i), 1)]).then_inc(job_hi, 1)
                        else:
                            n = LAST if i == KT - 1 else P
                            if i == 0:
                                act.wait_ge(pv_mm, at(t, NT, 0))
                            nc.scalar.activation(vh[0:n, i, :], src[0:n, 0:256], ACT.Copy).then_inc(job_hi, 1)
                    for g in range(NT):
                        h, i = divmod(g, KT)
                        n = LAST if i == KT - 1 else P
                        act.wait_ge(sc_mm, at(t, NT, g + 1))
                        act.wait_ge(sum_ok, at(t, HALVES * (KT - 1), sums_after(g - 2)))
                        act.wait_ge(lo_ok, at(t, NT, g - 1))
                        nc.scalar.activation(p32[0:n, g % 2, :], bank[(NJ + g) % RING][0:n, :], ACT.Exp,
                                             scale=XSCALE).then_inc(exp_ok, 1)
                        act.wait_ge(exp_ok, at(t, NT, g + 1))
                        act.wait_ge(pv_mm, at(t, NT, g - 1))
                        nc.scalar.activation(ph[0:n, g % 2, :], p32[0:n, g % 2, :], ACT.Copy).then_inc(hi_ok, 1)
                        if h == 1 and i in WKV_AT:
                            k = WKV_AT.index(i)
                            if k == 0:
                                act.wait_ge(stage_ld, 16 * (b * N_STAGE + p) + 16 * (N_STAGE + 6))
                                act.wait_ge(job, at(t, NJ, NJ))
                            high_part(wkvh[:, k, :], wstage[:, k, :])
                        if h >= 2 and i == 2:
                            add_bv(act, t, p, h - 2)
                        if h == HALVES - 1 and i == ends_at(h) + 5:
                            add_bv(act, t, p, h - 1)
                    add_bv(act, t, p, HALVES - 1)
                deviation(b, 1)
                copy_xt(b, 1)
                act.wait_ge(f_v, at(b, N_FV, 7))
                nc.scalar.activation(e21[:, :], dv21[:, :], ACT.Exp).then_inc(f_e, 1)
                for tb in range(TB):
                    act.wait_ge(f_t, at(b, TB, tb + 1))
                    for k, n in enumerate((P, ER - P)):
                        nc.scalar.activation(hgt[0:n, tb, k, :], pv[0:n, tb, k * P:(k + 1) * P], ACT.Copy).then_inc(f_tc, 1)
                deviation(b, 2)

        @block.vector
        def _(dve):
            for s_, n in ((ln, 3 * N_LN), (f_res, TB), (f_v, N_FV), (s_rope, N_ROPE), (s_qm, HB), (s_mx, 2 * HB), (s_rs, HB),
                          (s_pn, 2 * HB), (s_res, 2), (job_lo, NJ), (mx_free, MXU), (m4_ok, HALVES),
                          (shift_ok, HALVES), (lo_ok, NT), (rden_ok, 4 * HALVES), (on_ok, 2 * HALVES)):
                dve.sem_inc(s_, n)
            dve.wait_ge(c_ld, N_CONST)

            def layernorm(b, k, summed):
                def done(n):
                    dve.wait_ge(ln, at(b, 3 * N_LN, N_LN * k + n))
                for tb in range(TB):
                    summed(tb)
                    nc.vector.bn_stats(stats[:, tb, :], xres[:, tb, :]).then_inc(ln, 1)
                done(2)
                held(dve)
                for tb in range(TB):
                    nc.vector.bn_aggr(mv[:, tb, :], stats[:, tb, :]).then_inc(ln, 1)
                dve.wait_ge(ln_sd, at(b, 3, k + 1))
                nc.vector.reciprocal(rstd[:, :], rstd[:, :]).then_inc(ln, 1)
                done(5)
                for tb in range(TB):
                    nc.vector.tensor_scalar(xres[:, tb, :], xres[:, tb, :], mv[:, tb, 0:1], rstd[:, tb:tb + 1],
                                            ALU.subtract, ALU.mult).then_inc(ln, 1)

            with dve.Fori(0, nb) as b:
                dve.wait_ge(rp_ld, at(b, 16, 16))
                held(dve)
                with dve.Fori(0, NM) as m:
                    t = b * NM + m
                    for k, dst in enumerate((qr, kr)):
                        if k == 0:
                            dve.wait_ge(s_rope, at(t, N_ROPE, 0))
                            dve.wait_ge(s_qm, at(t, HB, 0))
                        else:
                            dve.wait_ge(s_rope, at(t, N_ROPE, 3))
                            dve.wait_ge(s_sc, at(t, HB, 0))
                        dve.wait_ge(s_qkb, at(t, 2, k + 1))
                        nc.vector.tensor_tensor(t1[:, :], qkb[:, k, :], rp[:, 0, :], ALU.mult).then_inc(s_rope, 1)
                        dve.wait_ge(s_qkv, at(t, 5, 3 + k))
                        nc.vector.tensor_tensor(t2[:, :], bank[k][:, S:2 * S], rp[:, 1, :], ALU.mult).then_inc(s_rope, 1)
                        dve.wait_ge(s_rope, at(t, N_ROPE, 3 * k + 2))
                        nc.vector.tensor_tensor(dst[:, :], t1[:, :], t2[:, :], ALU.add).then_inc(s_rope, 1)
                    dve.wait_ge(s_rope, at(t, N_ROPE, 3))

                    def one_head(h):
                        dve.wait_ge(s_sc, at(t, HB, h - 1))
                        nc.vector.tensor_scalar(qm[:, h % 2, :], qr[:, :], cst[:, C_HM + h:C_HM + h + 1], SSCALE,
                                                ALU.mult, ALU.mult).then_inc(s_qm, 1)
                    one_head(0)
                    one_head(1)
                    for h in range(HB + 1):
                        if h < HB:
                            dve.wait_ge(s_sc, at(t, HB, h + 1))
                            dve.wait_ge(s_exp, at(t, 2 * HB, 2 * h - 4))
                            for qb, (a, z) in enumerate(((0, 128), (128, 384))):
                                nc.vector.tensor_reduce(nmx[:, h % 3, qb:qb + 1], s_bank[h % 3][:, a:z], AX.X, ALU.max,
                                                        negate=True).then_inc(s_mx, 1)
                        if h + 2 < HB:
                            one_head(h + 2)
                        if h >= 1:
                            k = h - 1
                            dve.wait_ge(s_exp, at(t, 2 * HB, 2 * k + 2))
                            dve.wait_ge(s_pn, at(t, 2 * HB, 2 * k - 4))
                            nc.vector.reciprocal(rsm[:, k % 3, :], sm[:, k % 3, :]).then_inc(s_rs, 1)
                            dve.wait_ge(s_rs, at(t, HB, k + 1))
                            for qb, (a, z) in enumerate(((0, 128), (128, 384))):
                                nc.vector.tensor_scalar(pn[:, k % 3, a:z], pn[:, k % 3, a:z], rsm[:, k % 3, qb:qb + 1],
                                                        None, ALU.mult).then_inc(s_pn, 1)
                    dve.wait_ge(bias_ok, at(b, 2 * TB, TB))
                    for tb in range(TB):
                        dve.wait_ge(s_y, at(t, 2, tb + 1))
                        dve.wait_ge(s_res, at(t, 2, tb - 1))
                        nc.vector.tensor_tensor(xres[:, tb, :], xres[:, tb, :], mx[:, tb, :], ALU.add).then_inc(s_res, 1)
                layernorm(b, 0, lambda tb: dve.wait_ge(s_res, at(b * NM + (NM - 1), 2, tb + 1)))
                dve.wait_ge(bias_ok, at(b, 2 * TB, 2 * TB))
                held(dve)
                with dve.Fori(0, NP) as p:
                    t = b * NP + p

                    def reduce_pair(h, r):
                        k = h * (PAIRS + 1) + r
                        n = MCH[r % 2][2]
                        dve.wait_ge(mx_mm, at(t, HALVES * PAIRS, h * PAIRS + r + 1))
                        if r == 0:
                            dve.wait_ge(m4_ok, at(t, HALVES, h - 1))
                        nc.vector.tensor_reduce(mxp[:, h % 2, r:r + 1], mx[:, :, 0:n], AX.XY, ALU.max).then_inc(mx_free, 1)
                        assert k < MXU

                    def whole_max(h):
                        dve.wait_ge(mx_free, at(t, MXU, h * (PAIRS + 1) + PAIRS))
                        dve.wait_ge(mt_mm, at(t, HALVES, h - 1))
                        nc.vector.tensor_reduce(m4[:, h % 2, :], mxp[:, h % 2, :].rearrange("p (a c) -> p a c", c=2),
                                                AX.X, ALU.max).then_inc(m4_ok, 1)

                    def make_shift(h):
                        dve.wait_ge(mt_mm, at(t, HALVES, h + 1))
                        dve.wait_ge(sc_mm, at(t, NT, (h - 1) * KT))
                        nc.vector.tensor_tensor(shift[:, h % 2, :, :], blockm[:, :, :],
                                                mx[0:4, 0:1, 0:P].broadcast_to([4, 4, P]), ALU.mult).then_inc(shift_ok, 1)
                        dve.wait_ge(shift_ok, at(t, HALVES, h + 1))
                        dve.sem_inc(mx_free, 1)

                    for j, (kind, kv, i) in enumerate(JOBS):
                        if j in MAX_AT:
                            reduce_pair(0, MAX_AT.index(j))
                        if j == EARLY_AT:
                            reduce_pair(1, 0)
                        dve.wait_ge(job_hi, at(t, NJ, j + 1))
                        src = bank[j % RING]
                        if kind == "K":
                            a, n = KCH[i]
                            nc.vector.scalar_tensor_tensor(kl[:, kv, a:a + n], src[:, 0:n],
                                                           cst[:, bass.ds(2 * p + (C_BK + kv), 1)],
                                                           kh[:, kv, a:a + n], ALU.add, ALU.subtract).then_inc(job_lo, 1)
                        elif kind == "Q":
                            nc.vector.scalar_tensor_tensor(ql[:, kv, i * S:(i + 1) * S], src[:, 0:S],
                                                           cst[:, bass.ds(8 * p + (C_BQ + G * kv + i), 1)],
                                                           qh[:, kv, i * S:(i + 1) * S], ALU.add, ALU.subtract).then_inc(job_lo, 1)
                        else:
                            n = LAST if i == KT - 1 else P
                            nc.vector.tensor_tensor(vl[0:n, i, :], src[0:n, 0:256], vh[0:n, i, :],
                                                    ALU.subtract).then_inc(job_lo, 1)
                        if j == MAX_AT[-1]:
                            whole_max(0)
                        if j == MAX_AT[-1] + 2:
                            make_shift(0)

                    def reciprocals(h, q):
                        if q == 0:
                            dve.wait_ge(den_mm, at(t, HALVES, h + 1))
                            dve.wait_ge(on_ok, at(t, 2 * HALVES, 2 * h))
                        nc.vector.reciprocal(rden[:, q * P:(q + 1) * P], dn[:, q * P:(q + 1) * P]).then_inc(rden_ok, 1)

                    def normalize(h, k):
                        dve.wait_ge(rden_ok, at(t, 4 * HALVES, 4 * h + 2 * k + 2))
                        dve.wait_ge(pv_mm, at(t, NT, (h + 1) * KT))
                        dve.wait_ge(wo_used, at(t, 2 * G, 2 * h + k + 1 - 2 * G))
                        nc.vector.tensor_tensor(ot[:, 2 * h + k, :], pv[:, h % 2, k * S:(k + 1) * S],
                                                rden[:, k * S:(k + 1) * S], ALU.mult).then_inc(on_ok, 1)

                    reduce_pair(*pair_at(0))
                    for g in range(NT):
                        h, i = divmod(g, KT)
                        n = LAST if i == KT - 1 else P
                        if pair_at(g + 1):
                            reduce_pair(*pair_at(g + 1))
                        dve.wait_ge(hi_ok, at(t, NT, g + 1))
                        dve.wait_ge(pv_mm, at(t, NT, g - 1))
                        nc.vector.tensor_tensor(pl[0:n, g % 2, :], p32[0:n, g % 2, :], ph[0:n, g % 2, :],
                                                ALU.subtract).then_inc(lo_ok, 1)
                        if h + 1 < HALVES:
                            if i == PAIRS - 1:
                                whole_max(h + 1)
                            if i == PAIRS + 2:
                                make_shift(h + 1)
                        if h >= 1 and 0 <= i - ends_at(h) < 4:
                            reciprocals(h - 1, i - ends_at(h))
                        if h >= 1 and i == (KT - 1 if h < HALVES - 1 else ends_at(h) + 4):
                            normalize(h - 1, 0)
                            normalize(h - 1, 1)
                    for k in range(2):
                        reciprocals(HALVES - 1, 2 * k)
                        reciprocals(HALVES - 1, 2 * k + 1)
                        normalize(HALVES - 1, k)
                    dve.wait_ge(wo_used, at(t, 2 * G, 2 * G))
                    for tb in range(TB):
                        res = nc.vector.tensor_tensor(xres[:, tb, :], xres[:, tb, :], mx[:, tb, :], ALU.add)
                        res.then_inc(xr_ok, 1)
                    dve.wait_ge(xr_ok, t * 2 + 2)
                    dve.sem_inc(mx_free, 1)
                layernorm(b, 1, lambda tb: dve.wait_ge(xr_ok, (b * NP + NP) * 2 - 1 + tb))

                fv = [0]

                def step(ins):
                    ins.then_inc(f_v, 1)
                    fv[0] += 1

                def last():
                    dve.wait_ge(f_v, at(b, N_FV, fv[0]))
                dve.wait_ge(f_mm, at(b, TB, TB))
                step(nc.vector.tensor_copy(lg[:, :, :], mx[:, :, 0:NE]))
                last()
                held(dve)
                for tb in range(TB):
                    step(nc.vector.max(top8[:, tb, :], lg[:, tb, :]))
                last()
                held(dve)
                for tb in range(TB):
                    step(nc.vector.max_index(idx8[:, tb, :], top8[:, tb, :], lg[:, tb, :]))
                last()
                step(nc.vector.tensor_copy(idxf[:, :, :], idx8[:, :, :]))
                step(nc.vector.tensor_tensor(dv21[:, :], top8[:, :, 1], top8[:, :, 0], ALU.subtract))
                assert fv[0] == 7
                dve.wait_ge(f_e, at(b, 1, 1))
                step(nc.vector.tensor_scalar(den1[:, :], e21[:, :], 1.0, None, ALU.add))
                last()
                step(nc.vector.reciprocal(p1[:, :], den1[:, :]))
                last()
                step(nc.vector.tensor_scalar(p1s[:, :], p1[:, :], LORA_SCALING, None, ALU.mult))
                last()
                step(nc.vector.tensor_tensor(p2s[:, :], e21[:, :], p1s[:, :], ALU.mult))
                last()
                iota = cst[:, C_IOTA:C_IOTA + NE]
                for tb in range(TB):
                    for gk, ps, k in ((g1, p1s, 0), (g2, p2s, 1)):
                        step(nc.vector.tensor_scalar(gk[:, tb, :], iota, idxf[:, tb, k:k + 1], ps[:, tb:tb + 1],
                                                     ALU.is_equal, ALU.mult))
                last()
                step(nc.vector.tensor_tensor(gate[:, :, :], g1[:, :, :], g2[:, :, :], ALU.add))
                last()
                for tb in range(TB):
                    step(nc.vector.tensor_tensor(hg[:, tb, :].rearrange("p (e r) -> p e r", r=RANK),
                                                 mx[:, tb, NE:GA].rearrange("p (e r) -> p e r", r=RANK),
                                                 gate[:, tb, :].unsqueeze(2).broadcast_to([P, NE, RANK]), ALU.mult))
                assert fv[0] == N_FV, fv
                dve.wait_ge(f_o, at(b, TB, TB))
                for tb in range(TB):
                    nc.vector.tensor_tensor(xres[:, tb, :], xres[:, tb, :], bank[tb][:, :], ALU.add).then_inc(f_res, 1)
                layernorm(b, 2, lambda tb: dve.wait_ge(f_res, at(b, TB, tb + 1)))

        @block.tensor
        def _(pe):
            for s_, n in ((xt_ps, 4), (f_mm, TB), (f_base, 1), (f_t, TB), (f_o, TB), (s_qkv, 5), (s_sc, HB), (s_tp, HB), (s_pv, HB),
                          (s_y, 2), (wo_used, 2 * G), (job, NJ), (mx_mm, HALVES * PAIRS), (mt_mm, HALVES), (sc_mm, NT),
                          (pv_mm, NT), (den_mm, HALVES)):
                pe.sem_inc(s_, n)
            pe.wait_ge(c_ld, N_CONST)
            pe.wait_ge(c_set, 8)

            def mm(dst, lhs, rhs, first, final):
                return nc.tensor.matmul(dst, lhs, rhs, start=first, stop=final)

            def transpose_x(b, k):
                for tb in range(TB):
                    pe.wait_ge(ln, at(b, 3 * N_LN, N_LN * (k + 1) - (TB - 1) + tb))
                    for c in range(DC):
                        tr = nc.tensor.transpose(mx[:, tb, c * P:(c + 1) * P], xres[:, tb, c * P:(c + 1) * P], ident)
                    tr.then_inc(xt_ps, 1)

            with pe.Fori(0, nb) as b:
                pe.wait_ge(xt_ld, at(b, 16, 16))
                held(pe)
                pe.wait_ge(f_res, at(b, TB, 0))
                held(pe)
                with pe.Fori(0, NM) as m:
                    t = b * NM + m
                    pe.wait_ge(wq1_ld, at(t, 16, 16))
                    for kind in range(2):
                        for c in range(DC):
                            last = mm(bank[kind][:, 0:S], wqkv[:, kind * D + c * P:kind * D + (c + 1) * P], xt[:, c, :],
                                      c == 0, c == DC - 1)
                        last.then_inc(s_qkv, 1)

                    def project_v(tb):
                        for c in range(DC):
                            last = mm(dn[:, S + tb * P:S + (tb + 1) * P], xt[:, c, tb * P:(tb + 1) * P],
                                      wqkv[:, 2 * D + c * P:2 * D + (c + 1) * P], c == 0, c == DC - 1)
                        return last
                    pe.wait_ge(s_v, at(t, 2, 0))
                    for kind in range(2):
                        pe.wait_ge(s_qkb, at(t, 2, kind + 1))
                        mm(bank[kind][:, S:2 * S], swap[:, :], qkb[:, kind, :], True, True).then_inc(s_qkv, 1)
                        last = project_v(kind)
                    last.then_inc(s_qkv, 1)
                    pe.wait_ge(s_res, at(t, 2, 0))
                    pe.wait_ge(s_rope, at(t, N_ROPE, 6))
                    pe.wait_ge(s_ot, at(t, 1, 0))
                    for h in range(HB + 3):
                        if h < HB:
                            sc = s_bank[h % 3]
                            pe.wait_ge(s_qm, at(t, HB, h + 1))
                            pe.wait_ge(s_exp, at(t, 2 * HB, 2 * h - 4))
                            for qb, a in ((0, 0), (1, 128)):
                                w = (qb + 1) * P
                                mm(sc[:, a:a + w], qm[:, h % 2, qb * P:(qb + 1) * P], kr[:, 0:w], True, False)
                                last = mm(sc[:, a + w - P:a + w], identb[:, :], maskb[:, :], False, True)
                            last.then_inc(s_sc, 1)
                        if 2 <= h < HB + 2:
                            k = h - 2
                            pe.wait_ge(s_pn, at(t, 2 * HB, 2 * k + 2))
                            pe.wait_ge(s_ptc, at(t, HB, k - 1))
                            for a in (0, 128, 256):
                                last = nc.tensor.transpose(pv[:, k % 2, a:a + P], pn[:, k % 3, a:a + P], ident)
                            last.then_inc(s_tp, 1)
                        if h >= 3:
                            k = h - 3
                            pe.wait_ge(s_ptc, at(t, HB, k + 1))
                            pe.wait_ge(s_v, at(t, 2, 2))
                            mm(dn[:, 0:S], vx[:, 0, k * P:(k + 1) * P], pt[:, k % 2, 0:S], k == 0, False)
                            mm(dn[:, P:S], vx[:, 1, k * P:(k + 1) * P], pt[:, k % 2, S:S + P], False, k == HB - 1).then_inc(s_pv, 1)
                    pe.wait_ge(s_ot, at(t, 1, 1))
                    pe.wait_ge(wo1_ld, at(t, 16, 16))
                    for tb in range(TB):
                        mm(mx[:, tb, :], ots[:, tb * P:(tb + 1) * P], wos[:, 0:D], True, True).then_inc(s_y, 1)
                pe.wait_ge(s_res, at(b * NM + (NM - 1), 2, 2))
                transpose_x(b, 0)
                pe.wait_ge(split, at(b, N_STAGE, 5))
                held(pe)
                with pe.Fori(0, NP) as p:
                    t = b * NP + p
                    pe.wait_ge(split, at(b, N_STAGE, 5) + p)

                    def max_pair(h, r):
                        kv, q0 = h // 2, (h % 2) * QH + (r // 2) * P
                        pe.wait_ge(mx_free, at(t, MXU, h * (PAIRS + 1) + r))
                        for half in range(2):
                            a, n = MCH[r % 2][half]
                            last = mm(mx[:, half, 0:n], qh[:, kv, q0:q0 + P], kh[:, kv, a:a + n], True, True)
                        last.then_inc(mx_mm, 1)

                    def transpose_max(h):
                        pe.wait_ge(m4_ok, at(t, HALVES, h + 1))
                        mm(mx[0:4, 0, 0:P], m4[:, h % 2, :], ident, True, True).then_inc(mt_mm, 1)

                    for j, (kind, kv, i) in enumerate(JOBS):
                        if j in MAX_AT:
                            if j == MAX_AT[0]:
                                pe.wait_ge(job_lo, at(t, NJ, 8))
                            max_pair(0, MAX_AT.index(j))
                        if j == EARLY_AT:
                            max_pair(1, 0)
                        dst = bank[j % RING]
                        if j < RING:
                            pe.wait_ge(exp_ok, at(t, NT, j - RING + 1))
                        else:
                            pe.wait_ge(job_lo, at(t, NJ, j - RING + 1))
                        if kind == "K":
                            a, n = KCH[i]
                            w = slice(kv * P, (kv + 1) * P)
                            for c in range(DC):
                                mm(dst[:, 0:n], wkvh[:, c, w], ctxh[:, c, a:a + n], c == 0, False)
                                mm(dst[:, 0:n], wkvh[:, c, w], ctxl[:, c, a:a + n], False, False)
                                last = mm(dst[:, 0:n], wkvl[:, c, w], ctxh[:, c, a:a + n], False, c == DC - 1)
                        elif kind == "Q":
                            if i == 0:
                                pe.wait_ge(wq_ld, at(t, 32, 16 * (kv + 1)))
                                pe.wait_ge(xt_ok, at(b, 4, 2))
                            for c in range(DC):
                                last = mm(dst[:, 0:S], wqb[:, c, i * P:(i + 1) * P], xt[:, c, :], c == 0, c == DC - 1)
                        else:
                            n = LAST if i == KT - 1 else P
                            for c in range(DC):
                                keys = slice(i * P, i * P + n)
                                mm(dst[0:n, 0:256], ctxh[:, c, keys], wkvh[:, c, 256:512], c == 0, False)
                                mm(dst[0:n, 0:256], ctxh[:, c, keys], wkvl[:, c, 256:512], False, False)
                                last = mm(dst[0:n, 0:256], ctxl[:, c, keys], wkvh[:, c, 256:512], False, c == DC - 1)
                        last.then_inc(job, 1)
                        if j == MAX_AT[-1] + 2:
                            transpose_max(0)

                    def weigh(g):
                        h, i = divmod(g, KT)
                        kv, n = h // 2, LAST if i == KT - 1 else P
                        w = slice(kv * P, (kv + 1) * P)
                        if i == 0:
                            pe.wait_ge(on_ok, at(t, 2 * HALVES, 2 * (h - 1)))
                        pe.wait_ge(lo_ok, at(t, NT, g + 1))
                        dst = pv[:, h % 2, :]
                        mm(dst, vh[0:n, i, w], ph[0:n, g % 2, :], i == 0, False)
                        mm(dst, vh[0:n, i, w], pl[0:n, g % 2, :], False, False)
                        mm(dst, vl[0:n, i, w], ph[0:n, g % 2, :], False, i == KT - 1).then_inc(pv_mm, 1)

                    def denominators(h):
                        pe.wait_ge(sum_ok, at(t, HALVES * (KT - 1), (h + 1) * (KT - 1)))
                        pe.wait_ge(rden_ok, at(t, 4 * HALVES, 4 * h))
                        mm(dn[:, :], ones[:, :], psm[:, h % 2, :], True, True).then_inc(den_mm, 1)

                    def project(c, k):
                        if c == 0 and k == 0:
                            pe.wait_ge(mx_free, at(t, MXU, MXU - 1))
                        n = 2 * c + k
                        pe.wait_ge(wo_ld[n % 4], at(t, 32, 16 * (n // 4 + 1)))
                        pe.wait_ge(ot_ok, at(t, 2 * HALVES, 2 * c + k + 1))
                        for tb in range(TB):
                            last = mm(mx[:, tb, :], ot[:, n, tb * P:(tb + 1) * P], wob[:, n % 4, :],
                                      c == 0 and k == 0, c == 3 and k == 1)
                        last.then_inc(wo_used, 1)

                    for g in range(NT):
                        h, i = divmod(g, KT)
                        kv, q0 = h // 2, (h % 2) * QH
                        n = LAST if i == KT - 1 else P
                        keys, cols = slice(i * P, i * P + n), slice(q0, q0 + QH)
                        u = NJ + g
                        if pair_at(g):
                            max_pair(*pair_at(g))
                        dst = bank[u % RING][0:n, :]
                        if g < RING:
                            pe.wait_ge(job_lo, at(t, NJ, NJ + g - RING + 1))
                        else:
                            pe.wait_ge(exp_ok, at(t, NT, g - RING + 1))
                        if i == 0:
                            pe.wait_ge(shift_ok, at(t, HALVES, h + 1))
                        mm(dst, kh[:, kv, keys], qh[:, kv, cols], True, False)
                        mm(dst, kh[:, kv, keys], ql[:, kv, cols], False, False)
                        mm(dst, kl[:, kv, keys], qh[:, kv, cols], False, False)
                        mm(dst, negones[:, 0:n], shift[:, h % 2, :, :].rearrange("p a c -> p (a c)"), False, True).then_inc(sc_mm, 1)
                        if g >= 2:
                            weigh(g - 2)
                        if h + 1 < HALVES and i == PAIRS + 1:
                            transpose_max(h + 1)
                        if h == HALVES - 1 and i in (6, 8, 10):
                            project((i - 6) // 4, (i - 6) // 2 % 2)
                        if h >= 1 and i == 3:
                            denominators(h - 1)
                    weigh(NT - 2)
                    project(1, 1)
                    denominators(HALVES - 1)
                    weigh(NT - 1)
                    project(2, 0)
                    project(2, 1)
                    project(3, 0)
                    project(3, 1)
                transpose_x(b, 1)
                pe.wait_ge(f_ld, at(b, 48, 48))
                pe.wait_ge(xt_ok, at(b, 4, 4))
                for tb in range(TB):
                    rows = slice(tb * P, (tb + 1) * P)
                    for c in range(DC):
                        last = mm(mx[:, tb, 0:GA], xt[:, c, rows], wgat[:, c, :], c == 0, c == DC - 1)
                    last.then_inc(f_mm, 1)
                for tb in range(TB):
                    for c in range(DC):
                        last = mm(bank[tb][:, :], xt[:, c, tb * P:(tb + 1) * P], wbt[:, c, :], c == 0, False)
                last.then_inc(f_base, 1)
                pe.wait_ge(f_v, at(b, N_FV, N_FV))
                for tb in range(TB):
                    for k, n in enumerate((P, ER - P)):
                        last = nc.tensor.transpose(pv[0:n, tb, k * P:(k + 1) * P], hg[:, tb, k * P:k * P + n], ident)
                    last.then_inc(f_t, 1)
                for tb in range(TB):
                    pe.wait_ge(f_tc, at(b, 4, 2 * tb + 2))
                    mm(bank[tb][:, :], hgt[:, tb, 0, :], wlbt[:, 0, :], False, False)
                    mm(bank[tb][:, :], hgt[0:ER - P, tb, 1, :], wlbt[0:ER - P, 1, :], False, True).then_inc(f_o, 1)


_OUT = ((B, TB, P, D), "float32")


def kernel(**inputs):
    import concourse.bacc as bacc
    from concourse.bass_utils import run_bass_kernel_spmd

    nc = bacc.Bacc("TRN2", target_bir_lowering=False, num_devices=1)
    arrays = lay_out({k: np.asarray(v) for k, v in inputs.items()})
    args = {n: nc.dram_tensor(f"in_{n}", a.shape, mybir.dt.from_np(a.dtype), kind="ExternalInput").ap()
            for n, a in arrays.items()}
    o = nc.dram_tensor("out", (B, P, TB, D), F32, kind="ExternalOutput").ap()
    build(nc, **args, out=o)
    r = run_bass_kernel_spmd(nc, [{f"in_{n}": a for n, a in arrays.items()}], core_ids=[0])
    return np.ascontiguousarray(r.results[0]["out"].transpose(0, 2, 1, 3)).reshape(B, S, D)


def lay_out(i):
    c = np.ascontiguousarray
    kinds = [(i["L0_attn_Wq"], i["L0_attn_bq"]), (i["L0_attn_Wk"], i["L0_attn_bk"]), (i["L0_attn_Wv"], i["L0_attn_bv"])]
    ws = np.zeros((NM, P, W_QKV + D + 1), np.float32)
    for m in range(NM):
        rows = slice(m * P, (m + 1) * P)
        for k, (w, bias) in enumerate(kinds):
            ws[m, :, k * D:(k + 1) * D] = w[rows].T.reshape(DC, P, P).transpose(1, 0, 2).reshape(P, D)
            ws[m, :, 3 * D + k if k < 2 else W_QKV + D] = bias[rows]
        ws[m, :, W_QKV:W_QKV + D] = i["L0_attn_Wo"].T[rows]
    w = i["L0_xattn_Wkv"].reshape(DC, P, 2, NP, 2 * XD).transpose(3, 1, 0, 2, 4).reshape(NP, P, DC * 4 * XD)
    wkv = c(np.concatenate([w, w[:1]]))
    wq = c(i["L0_xattn_Wq"].reshape(DC, P, XKV, G * XD).transpose(2, 1, 0, 3))
    wo = c(i["L0_xattn_Wo"].reshape(XH, P, D))
    rows_b = lambda v: c(np.broadcast_to(v, (P, D)))
    wga = np.concatenate([i["L0_ffn_gate_W"], i["L0_ffn_lora_A"].reshape(ER, D)])
    wlb = np.zeros((2, P, D), np.float32)
    lb = i["L0_ffn_lora_B"].transpose(0, 2, 1).reshape(ER, D)
    wlb[0], wlb[1, :ER - P] = lb[:P], lb[P:]
    theta = (1.0 / 10000.0 ** (np.arange(0, DH, 2, dtype=np.float32) / DH)).astype(np.float32)
    ang = (np.arange(S, dtype=np.float32)[:, None] * theta[None, :]).astype(np.float32)
    d = np.arange(P) % DH
    sign = np.where(d % 2 == 0, -1.0, 1.0).astype(np.float32)
    rope = np.stack([np.cos(ang).T[d // 2], np.sin(ang).T[d // 2] * sign[:, None]], axis=1).astype(np.float32)
    consts = np.zeros((P, C_N), np.float32)
    consts[:, C_ID:C_ID + P] = np.eye(P)
    consts[:, C_SW:C_SW + P] = np.eye(P)[np.arange(P) ^ 1]
    consts[:, C_HM:C_HM + HB] = np.arange(P)[:, None] // DH == np.arange(HB)
    consts[:, C_IOTA:C_IOTA + NE] = np.arange(NE)
    consts[:, C_EPS] = EPS
    consts[:, C_BK:C_BK + XKV] = i["L0_xattn_bkv"][:XKV * XD].reshape(XKV, XD).T
    consts[:, C_BV:C_BV + XKV] = i["L0_xattn_bkv"][XKV * XD:].reshape(XKV, XD).T
    consts[:, C_BQ:C_BQ + XH] = i["L0_xattn_bq"].reshape(XH, XD).T
    bmask = c(np.broadcast_to(np.eye(4, dtype=np.float32)[:, :, None], (4, 4, P)))
    again = lambda v: c(np.concatenate([v, v[:1]]))
    return dict(
        x=again(i["x"].reshape(B, TB, P, D).transpose(0, 2, 1, 3)),
        x_t=again(i["x"].reshape(B, S, DC, P).transpose(0, 3, 2, 1)),
        ctx_t=c(i["ctx_4096"].reshape(B, LK, DC, P).transpose(0, 2, 3, 1)),
        ws=ws, wkv=wkv, wq=wq, wo=wo, bo_s=rows_b(i["L0_attn_bo"]), bo_x=rows_b(i["L0_xattn_bo"]),
        wb=c(i["L0_ffn_base_W"].T.reshape(DC, P, D).transpose(1, 0, 2)),
        wga=c(wga.T.reshape(DC, P, GA).transpose(1, 0, 2)), wlb=c(wlb.transpose(1, 0, 2)),
        rope=rope, consts=consts, bmask=bmask)
```
